# Optimizing a Trainium2 kernel written in Bass

```python
import numpy as np
import jax
import jax.numpy as jnp

def _softmax(x, axis=-1):
    return jax.nn.softmax(x, axis=axis)

def _gelu(x):
    return jax.nn.gelu(x, approximate=True)

def _silu(x):
    return jax.nn.silu(x)

def _sigmoid(x):
    return jax.nn.sigmoid(x)

def _layernorm(x, axis=-1, eps=1e-05):
    m = jnp.mean(x, axis=axis, keepdims=True)
    v = jnp.var(x, axis=axis, keepdims=True)
    return (x - m) / jnp.sqrt(v + eps)

def _scatter_add(tgt, idx, src, axis=0):
    return tgt.at[idx].add(src)

def _segment_sum(src, seg, n):
    return jax.ops.segment_sum(src, seg, n)
kernel_name = 'mk_decoder_preln_d1_seqx_r4_7ad2b5'

def setup_inputs(seed: int=0):
    np.random.seed(seed)
    _w = jnp.asarray

    def _rec_inputs():
        import jax
        import jax.numpy as jnp
        _rk = jax.random.key(seed)
        x = 7.22e-05 + 1 * jax.random.normal(jax.random.fold_in(_rk, 1), (16, 128, 256), jnp.float32)
        _lenS = 128 - jax.random.randint(jax.random.fold_in(_rk, 7), (16,), 0, max(1, 128 // 4) + 1, jnp.int32)
        _lenS2 = 128 - jax.random.randint(jax.random.fold_in(_rk, 8), (16,), 0, max(1, 128 // 4) + 1, jnp.int32)
        _ctx_1024P = jax.random.normal(jax.random.fold_in(_rk, 11), (16, 16, 256), jnp.float32)
        _ctx_1024c = jax.random.dirichlet(jax.random.fold_in(_rk, 511), 0.3 * jnp.ones((16,), jnp.float32), (16, 128))
        _ctx_1024t = jnp.einsum('bsk,bkd->bsd', _ctx_1024c, _ctx_1024P)
        _ctx_1024t = _ctx_1024t * jax.lax.rsqrt(jnp.mean(jnp.square(_ctx_1024t)) + 1e-12) * 0.953939
        ctx_1024 = 4.13588e-05 + 0.999923 * (_ctx_1024t + 0.3 * jax.random.normal(jax.random.fold_in(_rk, 611), (16, 128, 256), jnp.float32))
        return (x, ctx_1024)
    x, ctx_1024 = _rec_inputs()

    def _L0_attn_setup():
        import jax, jax.numpy as jnp
        import numpy as np
        NUM_HEADS = 16
        WINDOW = 64
        LN_EPS = 1e-05
        key = jax.random.key(seed)
        k1, k2, k3 = jax.random.split(key, 3)
        B, L, D = (2, 512, 256)
        x = jax.random.normal(k1, (B, L, D), dtype=jnp.float32)
        w_qkv = jax.random.normal(k2, (3 * D, D), dtype=jnp.float32) * 0.02
        w_out = jax.random.normal(k3, (D, D), dtype=jnp.float32) * 0.02
        gamma = jnp.ones((D,), dtype=jnp.float32)
        beta = jnp.zeros((D,), dtype=jnp.float32)
        return {'x': x, 'w_qkv': w_qkv, 'w_out': w_out, 'gamma': gamma, 'beta': beta}
    _L0_attn_all = _L0_attn_setup()
    _L0_attn_in = {k: v for k, v in _L0_attn_all.items() if k in ('w_qkv', 'w_out', 'gamma', 'beta')}
    del _L0_attn_all

    def _L0_xattn_setup():
        import jax, jax.numpy as jnp
        import numpy as np
        D_MODEL = 256
        NUM_HEADS = 16
        HEAD_DIM = D_MODEL // NUM_HEADS
        B, S = (4, 512)
        key = jax.random.key(seed)
        ks = jax.random.split(key, 6)
        scale = 1.0 / np.sqrt(D_MODEL)
        return {'q': jax.random.normal(ks[0], (B, S, D_MODEL), dtype=jnp.float32), 'k': jax.random.normal(ks[1], (B, S, D_MODEL), dtype=jnp.float32), 'v': jax.random.normal(ks[2], (B, S, D_MODEL), dtype=jnp.float32), 'Wq': jax.random.normal(ks[3], (D_MODEL, D_MODEL), dtype=jnp.float32) * scale, 'Wk': jax.random.normal(ks[4], (D_MODEL, D_MODEL), dtype=jnp.float32) * scale, 'Wv': jax.random.normal(ks[5], (D_MODEL, D_MODEL), dtype=jnp.float32) * scale}
    _L0_xattn_all = _L0_xattn_setup()
    _L0_xattn_in = {k: v for k, v in _L0_xattn_all.items() if k in ('Wq', 'Wk', 'Wv')}
    del _L0_xattn_all

    def _L0_ffn_setup():
        import jax, jax.numpy as jnp
        import numpy as np
        BLOCK = 32
        W_BITS = 4
        ACT_BITS = 16

        def act_qdq(x):
            qmax = 2.0 ** (ACT_BITS - 1) - 1.0
            scale = jnp.maximum(jnp.max(jnp.abs(x)) / qmax, 1e-12)
            return jnp.clip(jnp.round(x / scale), -qmax - 1.0, qmax) * scale

        def fixed_qdq_u16(x):
            scale = 1.0 / 65536.0
            return jnp.clip(jnp.round(x / scale), 0.0, 65535.0) * scale

        def lpbq_dequant(w):
            O, I = w.shape
            qmax = 2.0 ** (W_BITS - 1) - 1.0
            wb = w.reshape(O, I // BLOCK, BLOCK)
            s = jnp.maximum(jnp.max(jnp.abs(wb), axis=-1, keepdims=True) / qmax, 1e-12)
            wq = jnp.clip(jnp.round(wb / s), -qmax - 1.0, qmax) * s
            return wq.reshape(O, I)
        key = jax.random.key(seed)
        k1, k2, k3, k4 = jax.random.split(key, 4)
        B, S, H, I = (2, 1024, 256, 768)
        x = jax.random.normal(k1, (B, S, H), jnp.float32)
        w_gate = jax.random.normal(k2, (I, H), jnp.float32) * 0.02
        w_up = jax.random.normal(k3, (I, H), jnp.float32) * 0.02
        w_down = jax.random.normal(k4, (H, I), jnp.float32) * 0.02
        return {'x': x, 'w_gate': w_gate, 'w_up': w_up, 'w_down': w_down}
    _L0_ffn_all = _L0_ffn_setup()
    _L0_ffn_in = {k: v for k, v in _L0_ffn_all.items() if k in ('w_gate', 'w_up', 'w_down')}
    del _L0_ffn_all
    return {'x': x, 'ctx_1024': ctx_1024, 'L0_attn_w_qkv': _L0_attn_in['w_qkv'], 'L0_attn_w_out': _L0_attn_in['w_out'], 'L0_attn_gamma': _L0_attn_in['gamma'], 'L0_attn_beta': _L0_attn_in['beta'], 'L0_xattn_Wq': _L0_xattn_in['Wq'], 'L0_xattn_Wk': _L0_xattn_in['Wk'], 'L0_xattn_Wv': _L0_xattn_in['Wv'], 'L0_ffn_w_gate': _L0_ffn_in['w_gate'], 'L0_ffn_w_up': _L0_ffn_in['w_up'], 'L0_ffn_w_down': _L0_ffn_in['w_down']}

def reference(x, ctx_1024, L0_attn_w_qkv, L0_attn_w_out, L0_attn_gamma, L0_attn_beta, L0_xattn_Wq, L0_xattn_Wk, L0_xattn_Wv, L0_ffn_w_gate, L0_ffn_w_up, L0_ffn_w_down):
    import jax
    import jax.numpy as jnp

    def _L0_attn_ref(x, w_qkv, w_out, gamma, beta):
        import jax, jax.numpy as jnp
        import numpy as np
        NUM_HEADS = 16
        WINDOW = 64
        LN_EPS = 1e-05
        B, L, D = x.shape
        H = NUM_HEADS
        HD = D // H
        residual = x
        mu = jnp.mean(x, axis=-1, keepdims=True)
        var = jnp.mean(jnp.square(x - mu), axis=-1, keepdims=True)
        xn = (x - mu) * jax.lax.rsqrt(var + LN_EPS) * gamma + beta
        qkv = jnp.einsum('bld,ed->ble', xn, w_qkv).reshape(B, L, 3, H, HD)
        qkv = jnp.transpose(qkv, (2, 0, 3, 1, 4))
        q, k, v = (qkv[0], qkv[1], qkv[2])
        scores = jnp.einsum('bhqd,bhkd->bhqk', q, k) / jnp.sqrt(jnp.float32(HD))
        idx = jnp.arange(L)
        band = jnp.abs(idx[:, None] - idx[None, :]) <= WINDOW // 2
        scores = jnp.where(band[None, None], scores, -jnp.inf)
        attn = jax.nn.softmax(scores, axis=-1)
        out = jnp.einsum('bhqk,bhkd->bhqd', attn, v)
        out = jnp.transpose(out, (0, 2, 1, 3)).reshape(B, L, D)
        return residual + jnp.einsum('bld,ed->ble', out, w_out)

    def _L0_xattn_ref(q, k, v, Wq, Wk, Wv):
        import jax, jax.numpy as jnp
        import numpy as np
        D_MODEL = 256
        NUM_HEADS = 16
        HEAD_DIM = D_MODEL // NUM_HEADS
        B, S = (4, 512)
        b, s, d = q.shape
        qp = jnp.einsum('bsd,ed->bse', q, Wq)
        kp = jnp.einsum('bsd,ed->bse', k, Wk)
        vp = jnp.einsum('bsd,ed->bse', v, Wv)
        qh = qp.reshape(b, s, NUM_HEADS, HEAD_DIM).transpose(0, 2, 1, 3)
        kh = kp.reshape(b, s, NUM_HEADS, HEAD_DIM).transpose(0, 2, 1, 3)
        vh = vp.reshape(b, s, NUM_HEADS, HEAD_DIM).transpose(0, 2, 1, 3)
        scores = jnp.einsum('bhqd,bhkd->bhqk', qh, kh) / jnp.sqrt(jnp.float32(HEAD_DIM))
        attn = jax.nn.softmax(scores, axis=-1)
        att = jnp.einsum('bhqk,bhkd->bhqd', attn, vh)
        return att.reshape(b, s, d)

    def _L0_ffn_ref(x, w_gate, w_up, w_down):
        import jax, jax.numpy as jnp
        import numpy as np
        BLOCK = 32
        W_BITS = 4
        ACT_BITS = 16

        def act_qdq(x):
            qmax = 2.0 ** (ACT_BITS - 1) - 1.0
            scale = jnp.maximum(jnp.max(jnp.abs(x)) / qmax, 1e-12)
            return jnp.clip(jnp.round(x / scale), -qmax - 1.0, qmax) * scale

        def fixed_qdq_u16(x):
            scale = 1.0 / 65536.0
            return jnp.clip(jnp.round(x / scale), 0.0, 65535.0) * scale

        def lpbq_dequant(w):
            O, I = w.shape
            qmax = 2.0 ** (W_BITS - 1) - 1.0
            wb = w.reshape(O, I // BLOCK, BLOCK)
            s = jnp.maximum(jnp.max(jnp.abs(wb), axis=-1, keepdims=True) / qmax, 1e-12)
            wq = jnp.clip(jnp.round(wb / s), -qmax - 1.0, qmax) * s
            return wq.reshape(O, I)
        x = act_qdq(x)
        up = act_qdq(x @ lpbq_dequant(w_up).T)
        gate = act_qdq(x @ lpbq_dequant(w_gate).T)
        sig = fixed_qdq_u16(jax.nn.sigmoid(gate))
        gate = act_qdq(gate * sig)
        o = act_qdq(gate * up)
        return o @ lpbq_dequant(w_down).T
    x = x + _L0_attn_ref(_layernorm(x, axis=-1), L0_attn_w_qkv, L0_attn_w_out, L0_attn_gamma, L0_attn_beta)
    x = x + _L0_xattn_ref(_layernorm(x, axis=-1), ctx_1024, ctx_1024, L0_xattn_Wq, L0_xattn_Wk, L0_xattn_Wv)
    x = x + _L0_ffn_ref(_layernorm(x, axis=-1), L0_ffn_w_gate, L0_ffn_w_up, L0_ffn_w_down)
    return x

_drawn_inputs = setup_inputs


def setup_inputs(seed=0):
    import zlib

    import numpy as np

    out = dict(_drawn_inputs(seed))
    spreads = {'L0_attn_gamma': (1.0, 0.6), 'L0_attn_beta': (0.0, 0.8)}
    factors = {'L0_attn_w_qkv': 6.579,
     'L0_attn_w_out': 6.579,
     'L0_ffn_w_gate': 3.625,
     'L0_ffn_w_up': 3.336,
     'L0_ffn_w_down': 3.312}
    for name, (base, spread) in spreads.items():
        noise = np.random.default_rng([zlib.crc32(name.encode()), seed]).standard_normal(out[name].shape)
        drawn = base * np.exp(spread * noise) if base else spread * noise
        out[name] = jnp.asarray(drawn.astype(out[name].dtype))
    for name, factor in factors.items():
        out[name] = (out[name] * factor).astype(out[name].dtype)
    return out
```

```python
from contextlib import ExitStack

import numpy as np
import concourse.bass as bass
from concourse import mybir

F32 = mybir.dt.float32
BF16 = mybir.dt.bfloat16
ALU = mybir.AluOpType
ACT = mybir.ActivationFunctionType
AX_X = mybir.AxisListType.X

P = 128
D = 256
KT = D // P
HEADS = 16
HD = D // HEADS
WINDOW = 64
LN_EPS = 1e-5
FF = 768
BLOCK = 32
QMAX = 32767.0
WQMAX = 7.0
SIG_LEVELS = 65536.0
SCALE_FLOOR = 1e-12
ROUND = 12582912.0
MASKED = -1e38

NB = 16
TOK = NB * P
CB = 4
NCH = NB // CB
CT = CB * P
HU = HEADS // 2
UPI = 8
ITERS = NB * 2 // UPI
SLOTS = UPI // 2
SPLIT = 3
COMBOS = [(0, 1), (0, 0), (0, 2), (1, 0), (1, 1), (2, 0)]
STACK = len(COMBOS) * HD
NEG = STACK
VW = HD + 1
FT = FF // P

UNIT_HEADS = [[[HU * half + i for i in range(HU)] for half in range(2)],
              [[4 * (i % 4) + 2 * half + i // 4 for i in range(HU)] for half in range(2)]]


def stack_rows(side, part):
    at = [i for i, c in enumerate(COMBOS) if c[side] == part]
    step = at[1] - at[0] if len(at) > 1 else 1
    assert at == list(range(at[0], at[-1] + 1, step))
    return at[0], step, len(at)


def decoder_layer(nc, x, ctxT, wqkvT, woT, gamma, beta, xqT, xkT, xvT, w_gate, w_up, w_down, out):
    stacks = [[nc.dram_tensor(f"stack_{l}_{s}", [len(COMBOS), D, TOK], BF16, kind="Internal").ap()
               for s in range(2)] for l in range(2)]
    x_v = x.rearrange("(b p) d -> p b d", p=P)
    out_v = out.rearrange("(b p) d -> p b d", p=P)

    with ExitStack() as ctx:
        def sb(name, shape, dt=F32):
            return ctx.enter_context(nc.sbuf_tensor(name, shape, dt))

        def sem(name):
            return ctx.enter_context(nc.semaphore(name))

        resid = sb("resid", [P, NB, D])
        y = sb("y", [P, NB, D])
        w_qkv = sb("w_qkv", [P, KT, 3 * D])
        w_o = sb("w_o", [P, KT, D])
        w_x = sb("w_x", [P, 3, KT, D])
        gam = sb("gam", [P, KT])
        bet = sb("bet", [P, KT])
        w_gu = sb("w_gu", [P, 2 * FT, D])
        w_dn = sb("w_dn", [P, KT, FF])
        w_guT = sb("w_guT", [P, KT, 2 * FF])
        w_dnT = sb("w_dnT", [P, FT, D])
        x_intT = sb("x_intT", [P, KT, TOK])
        ident = sb("ident", [P, P])
        ident_b = sb("ident_b", [P, P], BF16)
        band = sb("band", [P, 4, P], BF16)
        zero = sb("zero", [P, HU])
        eps = sb("eps", [P, 1])
        rounder = sb("rounder", [P, 1])
        unrounder = sb("unrounder", [P, 1])
        stats = sb("stats", [P, NB, 6])
        mv = sb("mv", [P, NB, 2])
        sd = sb("sd", [P, NB])
        rstd = sb("rstd", [P, NB])
        nmr = sb("nmr", [P, NB])
        negm = sb("negm", [P, 4, HU])
        mparts = sb("mparts", [P, 4, SPLIT * HU], BF16)
        mrest = sb("mrest", [P, HU])
        m_T = sb("m_T", [SPLIT * HU, 4, P], BF16)
        attn = sb("attn", [P, 2, D])
        attnT = sb("attnT", [P, KT, P])
        rec = sb("rec", [P, 2, HEADS])
        o_tr = sb("o_tr", [P, 2 * P * 2])
        ablk = sb("ablk", [P, 2 * FT * 8 + KT * 24])
        wscale = sb("wscale", [P, 2 * FT * 8 + KT * 24])
        winv = sb("winv", [P, 2 * FT * 8 + KT * 24])
        tmax = sb("tmax", [P, NB])
        gmax = sb("gmax", [P, 6 * 4])
        umax = sb("umax", [P, 6 * 4])
        pmax = sb("pmax", [P, FT])
        omax = sb("omax", [P, FT])
        sc = sb("sc", [P, 32])

        arena_g = sb("arena_g", [P, FT * TOK])
        arena_u = sb("arena_u", [P, FT * TOK])
        gate = arena_g[:, :].rearrange("p (f k) -> p f k", f=FT)
        up = arena_u[:, :].rearrange("p (f k) -> p f k", f=FT)
        used = {"g": 0, "u": 0}

        def carve(which, words, dt=F32):
            a = {"g": arena_g, "u": arena_u}[which]
            at = used[which]
            used[which] = at + words
            assert at + words <= FT * TOK
            v = a[:, at:at + words]
            return v if dt == F32 else v.bitcast(dt)

        q_stk = carve("g", SLOTS * HEADS * P // 2, BF16).rearrange("p (s h k) -> p s h k", s=SLOTS, h=HEADS)
        k_stk = carve("g", SLOTS * HEADS * P // 2, BF16).rearrange("p (s h k) -> p s h k", s=SLOTS, h=HEADS)
        parts = carve("g", 4 * SPLIT * CT // 2, BF16).rearrange("p (j s k) -> p j s k", j=4, s=SPLIT)
        rest = carve("g", 2 * CT).rearrange("p (j k) -> p j k", j=2)
        v_all = carve("u", NB * HEADS * VW).rearrange("p (b h w) -> p b h w", b=NB, h=HEADS)
        v_slot = carve("u", SLOTS * HEADS * VW).rearrange("p (s h w) -> p s h w", s=SLOTS, h=HEADS)
        probT = carve("u", 2 * HU * P).rearrange("p (s h k) -> p s h k", s=2, h=HU)
        xT = carve("u", 2 * KT * CT).rearrange("p (s k t) -> p s k t", s=2, k=KT)
        cT = carve("u", 2 * KT * CT).rearrange("p (s k t) -> p s k t", s=2, k=KT)
        o_sb = carve("u", 2 * 2 * P).rearrange("p (s k) -> p s k", s=2)
        sig = y[:, :, :].rearrange("p (s b) d -> p s (b d)", s=2)

        bank = ctx.enter_context(nc.psum_tensor("bank", [P, 8, 512], F32))
        ps_s = bank[:, 0:2, :].rearrange("p b (h k) -> p (b h) k", h=4)
        ps_st = bank[:, 2:4, :].rearrange("p b (h k) -> p (b h) k", h=4)
        ps_pv = bank[:, 4, 0:2 * P]
        ps_ot = bank[:, 5, 0:2 * P]
        ps_mt = bank[:, 6, 0:P // 2].bitcast(BF16)
        ps_ap = bank[:, 7, :]

        x_landed = [sem(f"x_landed{c}") for c in range(NCH)]
        w1_landed = sem("w1_landed")
        w2_landed = sem("w2_landed")
        wf_landed = sem("wf_landed")
        ctx_landed = [sem(f"ctx_landed{i}") for i in range(2)]
        out_landed = sem("out_landed")
        consts = sem("consts")
        pool_init = sem("pool_init")
        band_half = sem("band_half")

        def layer_semaphores(l):
            names = ("xT_t", "xT_ready", "proj_done", "v_done", "v_ready", "hi_ready", "rest_ready", "mid_ready",
                     "lo_ready", "scores_done", "max_done", "mchain", "mparts_ready", "mT_done", "mT_ready",
                     "scoresT_done", "exp_done", "pv_done", "o_ready", "oT_done", "rec_ready", "norm_done",
                     "aT_done", "aT_ready", "outp_done", "resid_done", "stats_done", "mv_done",
                     "pv_zero")
            sems = {n: sem(f"l{l}_{n}") for n in names}
            sems["stored"] = [sem(f"l{l}_stored{j}") for j in range(4)]
            sems["qk_landed"] = [sem(f"l{l}_qk_landed{j}") for j in range(SLOTS)]
            sems["v_landed"] = [sem(f"l{l}_v_landed{j}") for j in range(SLOTS)]
            sems["neg_landed"] = [sem(f"l{l}_neg_landed{j}") for j in range(2)]
            return sems

        L = [layer_semaphores(l) for l in range(2)]

        bn_done = sem("bn_done")
        ln_stats = sem("ln_stats")
        ln_sd = sem("ln_sd")
        ln_link = sem("ln_link")
        ln_coef = sem("ln_coef")
        ln_apply = sem("ln_apply")
        ln_add = sem("ln_add")
        wq_abs = sem("wq_abs")
        wq_link = sem("wq_link")
        wq_scaled = sem("wq_scaled")
        wq_pool = sem("wq_pool")
        w_t = sem("w_t")
        w_ready = sem("w_ready")
        dve_link = sem("dve_link")
        x_abs = sem("x_abs")
        red_in = sem("red_in")
        red_out = sem("red_out")
        scale_ready = sem("scale_ready")
        xq = sem("xq")
        xq_t = sem("xq_t")
        xq_ready = sem("xq_ready")
        ff_done = sem("ff_done")
        ff_evac = sem("ff_evac")
        ff_abs = sem("ff_abs")
        g_round = sem("g_round")
        g_int = sem("g_int")
        sig_done = sem("sig_done")
        sig_round = sem("sig_round")
        sig_int = sem("sig_int")
        gs_done = sem("gs_done")
        gs_abs = sem("gs_abs")
        u_round = sem("u_round")
        u_int = sem("u_int")
        gs_round = sem("gs_round")
        o_done = sem("o_done")
        o_abs = sem("o_abs")
        o_round = sem("o_round")
        o_int = sem("o_int")
        down_done = sem("down_done")
        y_done = sem("y_done")

        block = ctx.enter_context(nc.Block())

        def when(eng, s, value):
            if not isinstance(value, int) or value > 0:
                eng.wait_ge(s, value)

        def run_steps(eng, step, before, after):
            for u in range(-before, UPI):
                step(0, u, lambda k: k >= 0)
            with eng.Fori(1, ITERS - 1) as it:
                for u in range(UPI):
                    step(it, u, lambda k: True)
            for u in range(UPI + after):
                step(ITERS - 1, u, lambda k: k < UPI)

        PARTS_OF = [[0, 1, 2, 3], [2, 3, 0, 1]]

        @block.sync
        def _(sp):
            for c in range(NCH):
                sp.dma_start(resid[:, c * CB:(c + 1) * CB, :], x_v[:, c * CB:(c + 1) * CB, :]).then_inc(x_landed[c], 16)
                if c == 0:
                    sp.dma_start(w_qkv[:, :, :], wqkvT.rearrange("(k p) n -> p k n", p=P)).then_inc(w1_landed, 16)
                    sp.dma_start(gam[:, :], gamma).then_inc(w1_landed, 16)
                    sp.dma_start(bet[:, :], beta).then_inc(w1_landed, 16)
            sp.dma_start(w_o[:, :, :], woT.rearrange("(k p) n -> p k n", p=P)).then_inc(w2_landed, 16)
            for i, w in enumerate((xqT, xkT, xvT)):
                sp.dma_start(w_x[:, i, :, :], w.rearrange("(k p) n -> p k n", p=P)).then_inc(w2_landed, 16)
            sp.dma_start(w_gu[:, 0:FT, :], w_gate.rearrange("(f p) n -> p f n", p=P)).then_inc(wf_landed, 16)
            sp.dma_start(w_gu[:, FT:2 * FT, :], w_up.rearrange("(f p) n -> p f n", p=P)).then_inc(wf_landed, 16)
            sp.dma_start(w_dn[:, :, :], w_down.rearrange("(f p) n -> p f n", p=P)).then_inc(wf_landed, 16)

            def load_ctx(c):
                if c >= 2:
                    sp.wait_ge(L[1]["proj_done"], 4 * (c - 2) + 2)
                    sp.wait_ge(L[1]["v_done"], 2 * (c - 2) + 2)
                sp.dma_start(cT[:, c % 2, :, :], ctxT[:, c * CT:(c + 1) * CT].rearrange("(k p) n -> p k n", p=P))\
                  .then_inc(ctx_landed[c % 2], 16)

            load_ctx(0)
            load_ctx(1)

            def store_parts(l, c):
                s = L[l]
                for pos, j in enumerate(PARTS_OF[l]):
                    n = 4 * c + pos
                    side, t = j // 2, j % 2
                    for part, ready in enumerate((s["hi_ready"], s["mid_ready"], s["lo_ready"])):
                        sp.wait_ge(ready, n + 1)
                        a, step, k = stack_rows(side, part)
                        dst = stacks[l][side][a:a + (k - 1) * step + 1:step, t * P:(t + 1) * P, c * CT:(c + 1) * CT]
                        sp.dma_start(dst.rearrange("c f k -> f c k"),
                                     parts[:, j, part:part + 1, :].to_broadcast([P, k, CT])).then_inc(s["stored"][j], 16)

            def stack_of(l, side, at):
                return stacks[l][side][:, :, at].rearrange("c (d h) k -> (c d) h k", h=HEADS)

            def load_qk(l, b, slot):
                at = bass.ds(b * P, P)
                sp.dma_start(q_stk[0:STACK, slot, :, :], stack_of(l, 0, at)).then_inc(L[l]["qk_landed"][slot], 16)
                sp.dma_start(k_stk[0:STACK, slot, :, :], stack_of(l, 1, at)).then_inc(L[l]["qk_landed"][slot], 16)

            def load_v(l, b, slot):
                sp.dma_start(v_slot[:, slot, :, :], v_all[:, bass.ds(b, 1), :, :].rearrange("p b h w -> p (b h) w"))\
                  .then_inc(L[l]["v_landed"][slot], 16)

            def attention(l):
                s = L[l]

                def step(it, u, exists):
                    if exists(u + 2):
                        sp.wait_ge(s["mT_ready"], it * UPI + u + 3)
                        v = u + 2
                        sp.dma_start(q_stk[NEG:NEG + SPLIT, (v // 2) % SLOTS, HU * (v % 2):HU * (v % 2) + HU, :],
                                     m_T[:, v % 4, :]).then_inc(s["neg_landed"][v % 2], 16)
                    if u >= 0 and u % 2 == 1 and exists(u + UPI):
                        b = it * SLOTS + (u // 2 + SLOTS)
                        sp.wait_ge(s["scoresT_done"], it * UPI + u + 1)
                        load_qk(l, b, u // 2)
                        sp.wait_ge(s["pv_done"], it * UPI + u + 1)
                        load_v(l, b, u // 2)

                run_steps(sp, step, 3, 0)

            for l in range(2):
                s = L[l]
                for c in range(NCH):
                    store_parts(l, c)
                    if l == 1 and c + 2 < NCH:
                        load_ctx(c + 2)
                    if c == 0:
                        for j in range(4):
                            sp.wait_ge(s["stored"][j], 16 * SPLIT)
                        sp.wait_ge(s["v_ready"], 2)
                        if l == 1:
                            sp.wait_ge(L[0]["pv_done"], 2 * NB)
                        for b in range(SLOTS):
                            load_qk(l, b, b)
                            load_v(l, b, b)
                for j in range(4):
                    sp.wait_ge(s["stored"][j], 16 * SPLIT * NCH)
                sp.wait_ge(s["v_ready"], 2 * NCH)
                attention(l)
            for c in range(NCH):
                sp.wait_ge(y_done, CB * (c + 1))
                sp.dma_start(out_v[:, c * CB:(c + 1) * CB, :], resid[:, c * CB:(c + 1) * CB, :]).then_inc(out_landed, 16)
            sp.wait_ge(out_landed, 16 * NCH)

        @block.gpsimd
        def _(pool):
            pool.memset(ident[:, :], 0.0).then_inc(pool_init, 1)
            pool.memset(ident_b[:, :], 0.0).then_inc(pool_init, 1)
            pool.memset(band[:, :, :], 0.0).then_inc(pool_init, 1)
            pool.wait_ge(pool_init, 3)
            for m in (ident, ident_b):
                pool.affine_select(out=m[:, :], in_=m[:, :], compare_op=ALU.not_equal, fill=1.0, base=0,
                                   pattern=[[-1, P]], channel_multiplier=1).then_inc(consts, 1)
            for sign in (1, -1):
                pool.affine_select(out=band[:, :, :], in_=band[:, :, :], compare_op=ALU.is_ge, fill=MASKED,
                                   base=WINDOW // 2, pattern=[[0, 4], [sign, P]], channel_multiplier=-sign)\
                    .then_inc(band_half if sign == 1 else consts, 1)
                if sign == 1:
                    pool.wait_ge(band_half, 1)
            pool.wait_ge(consts, 6)

            def apply(rnd, c):
                src = resid if rnd % 2 == 0 else y
                k = LN_ORDER.index((rnd, c))
                pool.wait_ge(ln_coef, k + 1)
                for b in range(c * CB, (c + 1) * CB):
                    pool.tensor_scalar(y[:, b, :], src[:, b, :], rstd[:, b:b + 1], nmr[:, b:b + 1],
                                       ALU.mult, ALU.add).then_inc(ln_apply, 1)

            def add_residual(c):
                pool.wait_ge(ln_apply, CB * (APPLY_ORDER.index((0, c)) + 1))
                for b in range(c * CB, (c + 1) * CB):
                    pool.tensor_tensor(resid[:, b, :], resid[:, b, :], y[:, b, :], ALU.add).then_inc(ln_add, 1)

            def mid_parts(l, c):
                for pos, j in enumerate(PARTS_OF[l]):
                    n = 4 * c + pos
                    pool.wait_ge(L[l]["rest_ready"], n + 1)
                    if c:
                        pool.wait_ge(L[l]["stored"][j], 16 * SPLIT * c)
                    pool.tensor_scalar(parts[:, j, 1, :], rest[:, n % 2, :], 1.0, None, ALU.mult)\
                        .then_inc(L[l]["mid_ready"], 1)

            def neg_parts(l):
                s = L[l]

                def step(it, u, exists):
                    if not exists(u + 3):
                        return
                    v = u + 3
                    n = it * UPI + v
                    m = negm[:, v % 4, :]
                    to = [mparts[:, v % 4, i * HU:(i + 1) * HU] for i in range(SPLIT)]
                    pool.wait_ge(s["max_done"], n + 1)
                    pool.tensor_tensor(to[0], m, zero[:, :], ALU.add).then_inc(s["mchain"], 1)
                    pool.wait_ge(s["mchain"], n * 3 + 1)
                    pool.tensor_tensor(mrest[:, :], m, to[0], ALU.subtract).then_inc(s["mchain"], 1)
                    pool.wait_ge(s["mchain"], n * 3 + 2)
                    pool.tensor_tensor(to[1], mrest[:, :], zero[:, :], ALU.add).then_inc(s["mchain"], 1)
                    pool.wait_ge(s["mchain"], n * 3 + 3)
                    pool.tensor_tensor(to[2], mrest[:, :], to[1], ALU.subtract).then_inc(s["mparts_ready"], 1)
                    pool.wait_ge(s["mparts_ready"], n + 1)

                run_steps(pool, step, 3, 0)

            for kind, rnd, c in POOL_PLAN:
                if kind == "apply":
                    apply(rnd, c)
                elif kind == "add":
                    add_residual(c)
                else:
                    mid_parts(0, c)
            neg_parts(0)

            for c in range(NCH):
                mid_parts(1, c)
                if c == 0:
                    pool.wait_ge(wq_scaled, 2)
                    for w, at, n in ((w_gu, 0, 2 * FT * 8), (w_dn, 2 * FT * 8, KT * 24)):
                        wv = w[:, :, :].rearrange("p f (g e) -> p (f g) e", e=BLOCK)
                        k = 3 * (at > 0)
                        pool.tensor_tensor(wv, wv, winv[:, at:at + n].unsqueeze(2).to_broadcast([P, n, BLOCK]), ALU.mult)\
                            .then_inc(wq_pool, 1)
                        pool.wait_ge(wq_pool, k + 1)
                        pool.tensor_scalar(wv, wv, ROUND, -ROUND, ALU.add, ALU.add).then_inc(wq_pool, 1)
                        pool.wait_ge(wq_pool, k + 2)
                        pool.tensor_tensor(wv, wv, wscale[:, at:at + n].unsqueeze(2).to_broadcast([P, n, BLOCK]), ALU.mult)\
                            .then_inc(wq_pool, 1)
            neg_parts(1)

            def all_max(k):
                pool.wait_ge(red_in, k + 1)
                pool.partition_all_reduce(sc[:, 2 * k + 1:2 * k + 2], sc[:, 2 * k:2 * k + 1], P,
                                          bass.bass_isa.ReduceOp.max).then_inc(red_out, 1)

            all_max(0)
            all_max(1)
            for f in range(FT):
                pool.wait_ge(g_round, f + 1)
                pool.tensor_scalar(gate[:, f, :], gate[:, f, :], -ROUND, None, ALU.add).then_inc(g_int, 1)
                pool.wait_ge(sig_round, f + 1)
                pool.tensor_scalar(sig[:, f % 2, :], sig[:, f % 2, :], ROUND + SIG_LEVELS - 1, -ROUND, ALU.min, ALU.add)\
                    .then_inc(sig_int, 1)
            all_max(2)
            all_max(3)
            for f in range(FT):
                pool.wait_ge(u_round, f + 1)
                pool.tensor_scalar(up[:, f, :], up[:, f, :], -ROUND, None, ALU.add).then_inc(u_int, 1)
            all_max(4)

        @block.scalar
        def _(act):
            act.wait_ge(consts, 6)

            def sqrt_var(rnd, c):
                a, b = c * CB, (c + 1) * CB
                act.wait_ge(ln_stats, CB * (LN_ORDER.index((rnd, c)) + 1))
                act.activation(sd[:, a:b], mv[:, a:b, 1], ACT.Sqrt, bias=eps[:, 0:1]).then_inc(ln_sd, 1)

            def evac_xT(l, c):
                s = L[l]
                act.wait_ge(s["xT_t"], c + 1)
                if c >= 2:
                    act.wait_ge(s["proj_done"], 4 * (c - 1))
                    act.wait_ge(s["v_done"], 2 * (c - 1))
                for k in range(KT):
                    if l == 0:
                        act.activation(xT[:, c % 2, k, :], bank[:, k, :], ACT.Identity, scale=gam[:, k:k + 1],
                                       bias=bet[:, k:k + 1]).then_inc(s["xT_ready"], 1)
                    else:
                        act.activation(xT[:, c % 2, k, :], bank[:, k, :], ACT.Copy).then_inc(s["xT_ready"], 1)

            def hi_parts(l, c, which):
                s = L[l]
                for pos, j in enumerate(PARTS_OF[l]):
                    if pos in which:
                        n = 4 * c + pos
                        act.wait_ge(s["proj_done"], n + 1)
                        if c:
                            act.wait_ge(s["stored"][j], 16 * SPLIT * c)
                        act.activation(parts[:, j, 0, :], bank[:, 2 + j, :], ACT.Copy).then_inc(s["hi_ready"], 1)

            def evac_v(l, c):
                s = L[l]
                for i in range(2):
                    b = c * CB + 2 * i
                    act.wait_ge(s["v_done"], 2 * c + i + 1)
                    act.activation(v_all[:, b:b + 2, :, 0:HD],
                                   bank[:, 6 + i, :].rearrange("p (b h w) -> p b h w", b=2, h=HEADS),
                                   ACT.Copy).then_inc(s["v_ready"], 1)

            def attention(l):
                s = L[l]

                def step(it, u, exists):
                    n = it * UPI + u
                    if u >= 0 and exists(u):
                        act.wait_ge(s["scoresT_done"], n + 1)
                        if exists(u - 2):
                            act.wait_ge(s["pv_done"], n - 1)
                        act.activation(probT[:, u % 2, :, :], ps_st, ACT.Exp, scale=HD ** -0.5)\
                            .then_inc(s["exp_done"], 1)
                    if l == 0 and exists(u - 1):
                        act.wait_ge(s["pv_done"], n)
                        if exists(u - 3):
                            act.wait_ge(s["oT_done"], n - 2)
                        act.activation(o_sb[:, (u - 1) % 2, :], ps_pv, ACT.Copy).then_inc(s["o_ready"], 1)
                    if exists(u + 2):
                        v = u + 2
                        act.wait_ge(s["mT_done"], n + 3)
                        act.activation(m_T[:, v % 4, :], ps_mt[0:SPLIT * HU, :], ACT.Copy).then_inc(s["mT_ready"], 1)
                    if l == 0 and u % 2 == 0 and exists(u - 4):
                        act.wait_ge(s["aT_done"], it * SLOTS + (u - 4) // 2 + 1)
                        act.activation(attnT[:, :, :], ps_ap[:, 0:D].rearrange("p (k t) -> p k t", k=KT), ACT.Copy)\
                            .then_inc(s["aT_ready"], 1)

                run_steps(act, step, 3, 5)

            act.wait_ge(w1_landed, 48)
            for kind, *a in ACT_PLAN:
                {"sqrt": sqrt_var, "xT": evac_xT, "v": evac_v, "hi": lambda l, c: hi_parts(l, c, range(4))}[kind](*a)
            attention(0)
            act.wait_ge(L[0]["mv_done"], NB)
            act.activation(sd[:, :], mv[:, :, 1], ACT.Sqrt, bias=eps[:, 0:1]).then_inc(ln_sd, 1)
            for c in range(NCH):
                hi_parts(1, c, (0, 1))
                evac_v(1, c)
                evac_xT(1, c)
                hi_parts(1, c, (2, 3))
            attention(1)
            act.wait_ge(L[1]["mv_done"], NB)
            act.activation(sd[:, :], mv[:, :, 1], ACT.Sqrt, bias=eps[:, 0:1]).then_inc(ln_sd, 1)
            for i in range(9):
                act.wait_ge(w_t, i + 1)
                if i < 6:
                    k, g = i // 3, i % 3
                    dst = w_guT[:, k, g * 512:(g + 1) * 512]
                else:
                    dst = w_dnT[:, 2 * (i - 6):2 * (i - 6) + 2, :].rearrange("p f n -> p (f n)")
                act.activation(dst, bank[:, i % 8, :], ACT.Copy).then_inc(w_ready, 1)
            for c in range(NCH):
                for k in range(KT):
                    n = c * KT + k
                    act.wait_ge(xq_t, n + 1)
                    act.activation(x_intT[:, k, c * CT:(c + 1) * CT], bank[:, (n + 1) % 8, :], ACT.Identity,
                                   bias=unrounder[:, 0:1]).then_inc(xq_ready, 1)

            def evac_ff(n):
                dst = (gate if n < 24 else up)[:, n % 6, (n // 6 % 4) * CT:(n // 6 % 4 + 1) * CT]
                act.wait_ge(ff_done, n + 1)
                act.activation(dst, bank[:, n % 8, :], ACT.Copy).then_inc(ff_evac, 1)

            for n in range(24):
                evac_ff(n)

            def round_gate(f):
                act.activation(gate[:, f, :], gate[:, f, :], ACT.Identity, scale=sc[:, 13:14], bias=rounder[:, 0:1])\
                    .then_inc(g_round, 1)

            for i in range(24):
                evac_ff(24 + i)
                f, ph = i // 4, i % 4
                if i == 2:
                    act.wait_ge(scale_ready, 2)
                    round_gate(0)
                if ph == 3:
                    act.wait_ge(g_int, f + 1)
                    if f >= 2:
                        act.wait_ge(gs_done, f - 1)
                    act.activation(sig[:, f % 2, :], gate[:, f, :], ACT.Sigmoid, scale=sc[:, 12:13]).then_inc(sig_done, 1)
                    if f + 1 < FT:
                        round_gate(f + 1)
                    act.wait_ge(sig_done, f + 1)
                    act.activation(sig[:, f % 2, :], sig[:, f % 2, :], ACT.Identity, scale=SIG_LEVELS,
                                   bias=rounder[:, 0:1]).then_inc(sig_round, 1)
            act.wait_ge(scale_ready, 3)
            for f in range(FT):
                act.activation(up[:, f, :], up[:, f, :], ACT.Identity, scale=sc[:, 15:16], bias=rounder[:, 0:1])\
                    .then_inc(u_round, 1)
                if f == 0:
                    act.wait_ge(scale_ready, 4)
                act.activation(gate[:, f, :], gate[:, f, :], ACT.Identity, scale=sc[:, 17:18], bias=rounder[:, 0:1])\
                    .then_inc(gs_round, 1)
            act.wait_ge(scale_ready, 5)
            for c in range(NCH):
                act.activation(up[:, :, c * CT:(c + 1) * CT], up[:, :, c * CT:(c + 1) * CT], ACT.Identity,
                               scale=sc[:, 19:20], bias=rounder[:, 0:1]).then_inc(o_round, 1)

        @block.tensor
        def _(pe):
            pe.wait_ge(consts, 6)

            def transpose_x(l, c):
                s = L[l]
                if l == 0:
                    pe.wait_ge(ln_apply, CB * (APPLY_ORDER.index((1, c)) + 1))
                else:
                    pe.wait_ge(ln_apply, CB * (2 * NCH + c + 1))
                when(pe, s["xT_ready"], KT * c)
                for k in range(KT):
                    for i in range(CB):
                        ins = pe.transpose(bank[:, k, i * P:(i + 1) * P], y[:, c * CB + i, k * P:(k + 1) * P], ident[:, :])
                ins.then_inc(s["xT_t"], 1)

            def project(l, c, which):
                s = L[l]
                for pos, j in enumerate(PARTS_OF[l]):
                    if pos not in which:
                        continue
                    n = 4 * c + pos
                    if c:
                        pe.wait_ge(s["rest_ready"], n - 3)
                    if l == 1 and j >= 2:
                        pe.wait_ge(ctx_landed[c % 2], 16 * (c // 2 + 1))
                        src = cT
                    else:
                        pe.wait_ge(s["xT_ready"], KT * (c + 1))
                        src = xT
                    for k in range(KT):
                        w = (w_qkv[:, k, j * P:(j + 1) * P] if l == 0 else
                             w_x[:, j // 2, k, (j % 2) * P:(j % 2 + 1) * P])
                        ins = pe.matmul(bank[:, 2 + j, :], w, src[:, c % 2, k, :], start=(k == 0), stop=(k == KT - 1))
                    ins.then_inc(s["proj_done"], 1)

            def values(l, c):
                s = L[l]
                src = xT if l == 0 else cT
                for i in range(CB):
                    if i % 2 == 0 and c:
                        pe.wait_ge(s["v_ready"], 2 * (c - 1) + i // 2 + 1)
                    for k in range(KT):
                        w = w_qkv[:, k, 2 * D:3 * D] if l == 0 else w_x[:, 2, k, :]
                        ins = pe.matmul(bank[:, 6 + i // 2, (i % 2) * D:(i % 2 + 1) * D],
                                        src[:, c % 2, k, i * P:(i + 1) * P], w, start=(k == 0), stop=(k == KT - 1))
                    if i % 2:
                        ins.then_inc(s["v_done"], 1)

            def attention(l):
                s = L[l]
                pe.wait_ge(s["xT_ready"], KT * NCH)
                pe.wait_ge(s["rest_ready"], 4 * NCH)
                pe.wait_ge(s["v_ready"], 2 * NCH)
                pe.wait_ge(s["pv_zero"], l + 1)

                def scores(it, u):
                    slot = (u // 2) % SLOTS
                    if u % 2 == 0:
                        pe.wait_ge(s["qk_landed"][slot], (it + u // UPI) * 32 + 32)
                    if not (isinstance(it, int) and it * UPI + u == 0):
                        pe.wait_ge(s["max_done"], it * UPI + u)
                    if l == 0:
                        for g in range(2):
                            pe.matmul(bank[:, g, :], ident_b[:, :], band[:, :, :].rearrange("p h k -> p (h k)"),
                                      start=True, stop=False, skip_group_check=True)
                    for i in range(HU):
                        h = HU * (u % 2) + i
                        ins = pe.matmul(ps_s[:, i, :], q_stk[0:STACK, slot, h, :], k_stk[0:STACK, slot, h, :],
                                        start=(l == 1), stop=True, skip_group_check=True)
                    ins.then_inc(s["scores_done"], 1)

                def scores_T(it, u):
                    slot = (u // 2) % SLOTS
                    pe.wait_ge(s["neg_landed"][u % 2], it * (16 * UPI // 2) + 16 * (u // 2 + 1))
                    if not (isinstance(it, int) and it * UPI + u == 0):
                        pe.wait_ge(s["exp_done"], it * UPI + u)
                    if l == 0:
                        for g in range(2):
                            pe.matmul(bank[:, 2 + g, :], ident_b[:, :], band[:, :, :].rearrange("p h k -> p (h k)"),
                                      start=True, stop=False, skip_group_check=True)
                    for i in range(HU):
                        h = HU * (u % 2) + i
                        ins = pe.matmul(ps_st[:, i, :], k_stk[0:NEG + SPLIT, slot, h, :], q_stk[0:NEG + SPLIT, slot, h, :],
                                        start=(l == 1), stop=True, skip_group_check=True)
                    ins.then_inc(s["scoresT_done"], 1)

                def weighted(it, u, has_before):
                    slot = (u // 2) % SLOTS
                    if u % 2 == 0:
                        pe.wait_ge(s["v_landed"][slot], (it + u // UPI) * 16 + 16)
                    pe.wait_ge(s["exp_done"], it * UPI + u + 1)
                    if has_before:
                        if l == 0:
                            pe.wait_ge(s["o_ready"], it * UPI + u)
                        elif u % 2 == 0:
                            pe.wait_ge(s["o_ready"], it * SLOTS + u // 2 - 1)
                    for i in range(HU):
                        h = UNIT_HEADS[l][u % 2][i]
                        r = 32 * (i % 4)
                        at = i // 4 * P + (l * (u % 2) * 2 * P)
                        out_bank = 4 + l * (u // 2 % 2)
                        ins = pe.matmul(bank[r:r + VW, out_bank, at:at + P], v_slot[:, slot, h, :],
                                        probT[:, u % 2, i, :], start=True, stop=True, skip_group_check=True)
                    ins.then_inc(s["pv_done"], 1)

                def step(it, u, exists):
                    n = it * UPI + u
                    if exists(u + 3):
                        scores(it, u + 3)
                    if u >= 0 and exists(u):
                        scores_T(it, u)
                    if exists(u - 1):
                        weighted(it, u - 1, exists(u - 2) if l == 0 else exists(u - 5))
                    if exists(u + 2):
                        v = u + 2
                        pe.wait_ge(s["mparts_ready"], n + 3)
                        if exists(u + 1):
                            pe.wait_ge(s["mT_ready"], n + 2)
                        pe.transpose(ps_mt[0:SPLIT * HU, :], mparts[:, v % 4, :], ident_b[:, :]).then_inc(s["mT_done"], 1)
                    if l == 0 and exists(u - 2):
                        v = u - 2
                        pe.wait_ge(s["o_ready"], n - 1)
                        if exists(u - 3):
                            pe.wait_ge(s["norm_done"], n - 2)
                        for g in range(2):
                            ins = pe.transpose(ps_ot[:, g * P:(g + 1) * P], o_sb[:, v % 2, g * P:(g + 1) * P], ident[:, :])
                        ins.then_inc(s["oT_done"], 1)
                    if l == 0 and u % 2 == 0 and exists(u - 4):
                        v = u - 4
                        nb = it * SLOTS + v // 2
                        pe.wait_ge(s["norm_done"], it * UPI + v + 2)
                        if exists(v - 2):
                            pe.wait_ge(s["resid_done"], nb)
                        for k in range(KT):
                            ins = pe.transpose(ps_ap[:, k * P:(k + 1) * P], attn[:, (v // 2) % 2, k * P:(k + 1) * P], ident[:, :])
                        ins.then_inc(s["aT_done"], 1)
                    if l == 0 and u % 2 == 1 and exists(u - 5):
                        nb = it * SLOTS + (u - 5) // 2
                        pe.wait_ge(s["aT_ready"], nb + 1)
                        for k in range(KT):
                            ins = pe.matmul(ps_ap[:, 0:D], attnT[:, k, :], w_o[:, k, :], start=(k == 0), stop=(k == KT - 1))
                        ins.then_inc(s["outp_done"], 1)

                run_steps(pe, step, 3, 6)

            pe.wait_ge(w1_landed, 48)
            transpose_x(0, 0)
            for c in range(NCH):
                project(0, c, range(4))
                if c + 1 < NCH:
                    transpose_x(0, c + 1)
                values(0, c)
            pe.wait_ge(w2_landed, 64)
            attention(0)
            pe.wait_ge(L[0]["max_done"], 2 * NB)
            pe.wait_ge(L[0]["exp_done"], 2 * NB)
            pe.wait_ge(L[0]["norm_done"], 2 * NB)
            pe.wait_ge(L[0]["resid_done"], NB)
            for c in range(NCH):
                project(1, c, (0, 1))
                values(1, c)
                transpose_x(1, c)
                project(1, c, (2, 3))
            attention(1)
            pe.wait_ge(L[1]["resid_done"], NB)
            pe.wait_ge(wq_pool, 6)
            for i in range(9):
                if i == 8:
                    pe.wait_ge(w_ready, 1)
                for j in range(4):
                    if i < 6:
                        k, f = i // 3, (i % 3) * 4 + j
                        src = w_gu[:, f, k * P:(k + 1) * P]
                    else:
                        f, k = 2 * (i - 6) + j // 2, j % 2
                        src = w_dn[:, k, f * P:(f + 1) * P]
                    ins = pe.transpose(bank[:, i % 8, j * P:(j + 1) * P], src, ident[:, :])
                ins.then_inc(w_t, 1)
            for c in range(NCH):
                pe.wait_ge(xq, c + 1)
                for k in range(KT):
                    n = c * KT + k
                    pe.wait_ge(w_ready, min(9, n + 2))
                    for i in range(CB):
                        ins = pe.transpose(bank[:, (n + 1) % 8, i * P:(i + 1) * P], y[:, c * CB + i, k * P:(k + 1) * P], ident[:, :])
                    ins.then_inc(xq_t, 1)
            pe.wait_ge(w_ready, 9)
            for n in range(48):
                which, c, f = n // 24, n // 6 % 4, n % 6
                pe.wait_ge(xq_ready, KT * NCH if n < 24 else 1)
                if n >= 8:
                    pe.wait_ge(ff_evac, n - 7)
                for k in range(KT):
                    ins = pe.matmul(bank[:, n % 8, :], w_guT[:, k, which * FF + f * P:which * FF + (f + 1) * P],
                                    x_intT[:, k, c * CT:(c + 1) * CT], start=(k == 0), stop=(k == KT - 1))
                ins.then_inc(ff_done, 1)
            pe.wait_ge(ff_evac, 48)
            for b in range(NB):
                pe.wait_ge(o_int, b // CB + 1)
                if b >= 8:
                    pe.wait_ge(y_done, b - 7)
                for f in range(FT):
                    ins = pe.matmul(bank[:, b % 8, 0:D], up[:, f, b * P:(b + 1) * P], w_dnT[:, f, :],
                                    start=(f == 0), stop=(f == FT - 1))
                ins.then_inc(down_done, 1)

        @block.vector
        def _(dve):
            dve.memset(eps[:, :], LN_EPS).then_inc(dve_link, 1)
            dve.memset(rounder[:, :], ROUND).then_inc(dve_link, 1)
            dve.memset(unrounder[:, :], -ROUND).then_inc(dve_link, 1)
            dve.memset(k_stk[NEG:NEG + SPLIT, :, :, :], 1.0).then_inc(consts, 1)
            dve.memset(v_all[:, :, :, HD:VW], 1.0).then_inc(consts, 1)
            dve.memset(zero[:, :], 0.0).then_inc(consts, 1)
            dve.wait_ge(dve_link, 3)
            chain = [3]

            def link(ins):
                chain[0] += 1
                ins.then_inc(dve_link, 1)
                dve.wait_ge(dve_link, chain[0])

            def norm_stats(rnd, c):
                src = resid if rnd == 0 else y
                k = LN_ORDER.index((rnd, c))
                if rnd == 0:
                    dve.wait_ge(x_landed[c], 16)
                else:
                    dve.wait_ge(ln_apply, CB * (APPLY_ORDER.index((0, c)) + 1))
                    dve.wait_ge(ln_coef, LN_ORDER.index((0, c)) + 1)
                for b in range(c * CB, (c + 1) * CB):
                    dve.bn_stats(stats[:, b, :], src[:, b, :]).then_inc(bn_done, 1)
                dve.wait_ge(bn_done, CB * (k + 1))
                for b in range(c * CB, (c + 1) * CB):
                    dve.bn_aggr(mv[:, b, :], stats[:, b, :]).then_inc(ln_stats, 1)

            def norm_coef(k, a, b):
                dve.wait_ge(ln_sd, k + 1)
                dve.reciprocal(rstd[:, a:b], sd[:, a:b]).then_inc(ln_link, 1)
                dve.wait_ge(ln_link, k + 1)
                dve.scalar_tensor_tensor(out=nmr[:, a:b], in0=mv[:, a:b, 0], scalar=-1.0, in1=rstd[:, a:b],
                                         op0=ALU.mult, op1=ALU.mult).then_inc(ln_coef, 1)

            def low_part(l, n):
                s = L[l]
                j = PARTS_OF[l][n % 4]
                dve.wait_ge(s["mid_ready"], n + 1)
                dve.tensor_tensor(parts[:, j, 2, :], rest[:, n % 2, :], parts[:, j, 1, :], ALU.subtract)\
                   .then_inc(s["lo_ready"], 1)

            def split(l, c, which):
                s = L[l]
                for pos, j in enumerate(PARTS_OF[l]):
                    if pos not in which:
                        continue
                    n = 4 * c + pos
                    dve.wait_ge(s["hi_ready"], n + 1)
                    if n >= 2:
                        dve.wait_ge(s["lo_ready"], n - 1)
                    dve.tensor_tensor(rest[:, n % 2, :], bank[:, 2 + j, :], parts[:, j, 0, :], ALU.subtract)\
                       .then_inc(s["rest_ready"], 1)
                    if n:
                        low_part(l, n - 1)

            def residual_stats(s, nb):
                dve.wait_ge(s["resid_done"], nb + 1)
                dve.bn_stats(stats[:, bass.ds(nb, 1), :], resid[:, bass.ds(nb, 1), :]).then_inc(s["stats_done"], 1)

            def all_moments(s):
                dve.wait_ge(s["stats_done"], NB)
                for b in range(NB):
                    dve.bn_aggr(mv[:, b, :], stats[:, b, :]).then_inc(s["mv_done"], 1)

            def attention(l):
                s = L[l]
                dve.wait_ge(s["rest_ready"], 4 * NCH)
                dve.wait_ge(s["proj_done"], 4 * NCH)
                for i in range(l + 1):
                    dve.memset(bank[:, 4 + i, :], 0.0).then_inc(s["pv_zero"], 1)

                def step(it, u, exists):
                    n = it * UPI + u
                    if exists(u + 3):
                        v = u + 3
                        dve.wait_ge(s["scores_done"], n + 4)
                        dve.tensor_reduce(negm[:, v % 4, :], ps_s, AX_X, ALU.max, negate=True).then_inc(s["max_done"], 1)
                    if l == 0 and exists(u - 2):
                        v = u - 2
                        hs = HU * (v % 2)
                        dve.wait_ge(s["oT_done"], n - 1)
                        ot = ps_ot.rearrange("p (h w) -> p h w", h=HU)
                        dve.reciprocal(rec[:, v % 2, 0:HU], ot[:, :, HD]).then_inc(s["rec_ready"], 1)
                        dve.wait_ge(s["rec_ready"], n - 1)
                        if exists(v - 4):
                            dve.wait_ge(s["aT_done"], it * SLOTS + v // 2 - 1)
                        dst = attn[:, (v // 2) % 2, hs * HD:(hs + HU) * HD]
                        dve.tensor_tensor(dst.rearrange("p (h w) -> p h w", h=HU), ot[:, :, 0:HD],
                                          rec[:, v % 2, 0:HU].unsqueeze(2).to_broadcast([P, HU, HD]), ALU.mult)\
                           .then_inc(s["norm_done"], 1)
                    if l == 1 and u % 2 == 0 and exists(u - 1):
                        v = u - 2
                        nb = it * SLOTS + v // 2
                        dve.wait_ge(s["pv_done"], n)
                        src = bank[:, 4 + v // 2 % 2, :].rearrange("p (g j i) -> p i g j", g=4, j=HU)
                        dve.transpose(o_tr[:, :], src).then_inc(s["o_ready"], 1)
                        dve.wait_ge(s["o_ready"], nb + 1)
                        ot = o_tr[:, :].rearrange("p (i w) -> p i w", w=32)
                        dve.reciprocal(rec[:, 0, :], ot[:, :, HD]).then_inc(s["rec_ready"], 1)
                        dve.wait_ge(s["rec_ready"], nb + 1)
                        dst = attn[:, 0, :]
                        dve.tensor_tensor(dst.rearrange("p (i w) -> p i w", w=HD), ot[:, :, 0:HD],
                                          rec[:, 0, :].unsqueeze(2).to_broadcast([P, HEADS, HD]), ALU.mult)\
                           .then_inc(s["norm_done"], 1)
                        dve.wait_ge(s["norm_done"], nb + 1)
                        r = resid[:, bass.ds(nb, 1), :].rearrange("p b w -> p (b w)")
                        dve.tensor_tensor(r, r, dst, ALU.add).then_inc(s["resid_done"], 1)
                        residual_stats(s, nb)
                    if l == 0 and u % 2 == 1 and exists(u - 5):
                        nb = it * SLOTS + (u - 5) // 2
                        dve.wait_ge(s["outp_done"], nb + 1)
                        r = resid[:, bass.ds(nb, 1), :].rearrange("p b w -> p (b w)")
                        dve.tensor_tensor(r, ps_ap[:, 0:D], r, ALU.add).then_inc(s["resid_done"], 1)
                        residual_stats(s, nb)

                run_steps(dve, step, 3, 6)

            for kind, *a in DVE_PLAN:
                if kind == "stats":
                    norm_stats(*a)
                elif kind == "coef":
                    rnd, c = a
                    norm_coef(LN_ORDER.index((rnd, c)), c * CB, (c + 1) * CB)
                else:
                    split(0, a[0], range(4))
            low_part(0, 4 * NCH - 1)
            dve.wait_ge(ln_add, NB)
            attention(0)
            all_moments(L[0])
            norm_coef(2 * NCH, 0, NB)
            dve.wait_ge(ln_coef, 2 * NCH + 1)

            def apply(c):
                for b in range(c * CB, (c + 1) * CB):
                    dve.tensor_scalar(y[:, b, :], resid[:, b, :], rstd[:, b:b + 1], nmr[:, b:b + 1], ALU.mult, ALU.add)\
                       .then_inc(ln_apply, 1)

            apply(0)
            dve.wait_ge(wf_landed, 48)
            for w, at, n in ((w_gu, 0, 2 * FT * 8), (w_dn, 2 * FT * 8, KT * 24)):
                dve.tensor_reduce(ablk[:, at:at + n], w[:, :, :].rearrange("p f (g e) -> p (f g) e", e=BLOCK), AX_X,
                                  ALU.max, apply_absolute_value=True).then_inc(wq_abs, 1)
            dve.wait_ge(wq_abs, 2)
            dve.tensor_scalar(wscale[:, :], ablk[:, :], 1.0 / WQMAX, SCALE_FLOOR, ALU.mult, ALU.max).then_inc(wq_scaled, 1)
            dve.wait_ge(wq_scaled, 1)
            dve.reciprocal(winv[:, :], wscale[:, :]).then_inc(wq_scaled, 1)
            for c in range(NCH):
                split(1, c, (0, 1))
                if c + 1 < NCH:
                    apply(c + 1)
                split(1, c, (2, 3))
            low_part(1, 4 * NCH - 1)
            attention(1)
            all_moments(L[1])
            norm_coef(2 * NCH + 1, 0, NB)
            dve.wait_ge(ln_coef, 2 * NCH + 2)
            for b in range(NB):
                dve.tensor_scalar(y[:, b, :], resid[:, b, :], rstd[:, b:b + 1], nmr[:, b:b + 1], ALU.mult, ALU.add)\
                   .then_inc(ln_apply, 1)
            dve.wait_ge(ln_apply, CB * 4 * NCH)
            link(dve.tensor_reduce(tmax[:, :], y[:, :, :], AX_X, ALU.max, apply_absolute_value=True))

            def quant_scale(k, cells, prefactor):
                dve.tensor_reduce(sc[:, 2 * k:2 * k + 1], cells, AX_X, ALU.max).then_inc(red_in, 1)
                dve.wait_ge(red_out, k + 1)
                s_, m_ = sc[:, 10 + 2 * k:11 + 2 * k], sc[:, 11 + 2 * k:12 + 2 * k]
                if prefactor is None:
                    link(dve.tensor_scalar(s_, sc[:, 2 * k + 1:2 * k + 2], 1.0 / QMAX, SCALE_FLOOR, ALU.mult, ALU.max))
                    dve.reciprocal(m_, s_).then_inc(scale_ready, 1)
                else:
                    link(dve.tensor_scalar(sc[:, 24:25], sc[:, 2 * k + 1:2 * k + 2], prefactor, 1.0 / QMAX, ALU.mult, ALU.mult))
                    link(dve.tensor_scalar(s_, sc[:, 24:25], SCALE_FLOOR, None, ALU.max))
                    link(dve.reciprocal(sc[:, 25:26], s_))
                    dve.tensor_scalar(m_, sc[:, 25:26], prefactor, None, ALU.mult).then_inc(scale_ready, 1)
                dve.wait_ge(scale_ready, k + 1)

            quant_scale(0, tmax[:, :], None)
            for c in range(NCH):
                yc = y[:, c * CB:(c + 1) * CB, :]
                dve.tensor_scalar(yc, yc, sc[:, 11:12], ROUND, ALU.mult, ALU.add).then_inc(xq, 1)

            def abs_ff(n):
                src = (gate if n < 24 else up)[:, n % 6, (n // 6 % 4) * CT:(n // 6 % 4 + 1) * CT]
                dve.wait_ge(ff_evac, n + 1)
                dve.tensor_reduce((gmax if n < 24 else umax)[:, n % 24:n % 24 + 1], src, AX_X, ALU.max,
                                  apply_absolute_value=True).then_inc(ff_abs, 1)

            for n in range(24):
                abs_ff(n)
            dve.wait_ge(ff_abs, 24)
            quant_scale(1, gmax[:, :], sc[:, 10:11])
            for i in range(24):
                abs_ff(24 + i)
                if i % 4 == 3:
                    f = i // 4
                    dve.wait_ge(sig_int, f + 1)
                    dve.tensor_tensor(gate[:, f, :], gate[:, f, :], sig[:, f % 2, :], ALU.mult).then_inc(gs_done, 1)
                    dve.wait_ge(gs_done, f + 1)
                    dve.tensor_reduce(pmax[:, f:f + 1], gate[:, f, :], AX_X, ALU.max, apply_absolute_value=True)\
                       .then_inc(gs_abs, 1)
            dve.wait_ge(ff_abs, 48)
            quant_scale(2, umax[:, :], sc[:, 10:11])
            link(dve.tensor_scalar(sc[:, 26:27], sc[:, 12:13], 1.0 / SIG_LEVELS, None, ALU.mult))
            dve.wait_ge(gs_abs, FT)
            quant_scale(3, pmax[:, :], sc[:, 26:27])
            for f in range(FT):
                dve.wait_ge(gs_round, f + 1)
                dve.wait_ge(u_int, f + 1)
                dve.scalar_tensor_tensor(out=up[:, f, :], in0=gate[:, f, :], scalar=-ROUND, in1=up[:, f, :],
                                         op0=ALU.add, op1=ALU.mult).then_inc(o_done, 1)
                dve.wait_ge(o_done, f + 1)
                dve.tensor_reduce(omax[:, f:f + 1], up[:, f, :], AX_X, ALU.max, apply_absolute_value=True)\
                   .then_inc(o_abs, 1)
            link(dve.tensor_scalar(sc[:, 27:28], sc[:, 14:15], sc[:, 16:17], None, ALU.mult))
            dve.wait_ge(o_abs, FT)
            quant_scale(4, omax[:, :], sc[:, 27:28])

            def final(b):
                dve.wait_ge(down_done, b + 1)
                dve.scalar_tensor_tensor(out=resid[:, b, :], in0=bank[:, b % 8, 0:D], scalar=sc[:, 18:19],
                                         in1=resid[:, b, :], op0=ALU.mult, op1=ALU.add).then_inc(y_done, 1)

            for c in range(NCH):
                oc = up[:, :, c * CT:(c + 1) * CT]
                dve.wait_ge(o_round, c + 1)
                dve.tensor_scalar(oc, oc, -ROUND, None, ALU.add).then_inc(o_int, 1)
                if c:
                    for b in range((c - 1) * CB, c * CB):
                        final(b)
            for b in range((NCH - 1) * CB, NB):
                final(b)


LN_ORDER = [(0, 0), (0, 1), (0, 2), (1, 0), (0, 3), (1, 1), (1, 2), (1, 3)]
DVE_PLAN = [("stats", 0, 0), ("stats", 0, 1), ("coef", 0, 0), ("stats", 0, 2), ("coef", 0, 1), ("stats", 1, 0),
            ("coef", 0, 2), ("stats", 0, 3), ("coef", 1, 0), ("stats", 1, 1), ("coef", 0, 3), ("coef", 1, 1),
            ("split", 0), ("stats", 1, 2), ("coef", 1, 2), ("split", 1), ("stats", 1, 3), ("coef", 1, 3),
            ("split", 2), ("split", 3)]
POOL_PLAN = [("apply", 0, 0), ("apply", 0, 1), ("add", 0, 0), ("apply", 0, 2), ("apply", 1, 0), ("add", 0, 1),
             ("apply", 0, 3), ("apply", 1, 1), ("add", 0, 2), ("add", 0, 3), ("mid", 0, 0), ("apply", 1, 2),
             ("mid", 0, 1), ("apply", 1, 3), ("mid", 0, 2), ("mid", 0, 3)]
APPLY_ORDER = [(r, c) for k, r, c in POOL_PLAN if k == "apply"]
ACT_PLAN = [("sqrt", 0, 0), ("sqrt", 0, 1), ("sqrt", 0, 2), ("sqrt", 1, 0), ("sqrt", 0, 3), ("sqrt", 1, 1),
            ("xT", 0, 0), ("hi", 0, 0), ("xT", 0, 1), ("v", 0, 0), ("sqrt", 1, 2), ("hi", 0, 1), ("xT", 0, 2),
            ("v", 0, 1), ("sqrt", 1, 3), ("hi", 0, 2), ("xT", 0, 3), ("v", 0, 2), ("hi", 0, 3), ("v", 0, 3)]


def by_dim(w, layer):
    heads = [h for half in UNIT_HEADS[layer] for h in half]
    return w.reshape(HEADS, HD, D)[heads].transpose(2, 1, 0).reshape(D, D)


def kernel(x, ctx_1024, L0_attn_w_qkv, L0_attn_w_out, L0_attn_gamma, L0_attn_beta, L0_xattn_Wq, L0_xattn_Wk,
           L0_xattn_Wv, L0_ffn_w_gate, L0_ffn_w_up, L0_ffn_w_down):
    import concourse.bacc as bacc
    from concourse.bass_utils import run_bass_kernel_spmd

    wqkv = np.asarray(L0_attn_w_qkv)
    laid = {
        "x": np.asarray(x).reshape(TOK, D),
        "ctxT": np.asarray(ctx_1024).reshape(TOK, D).T,
        "wqkvT": np.concatenate([by_dim(wqkv[0:D], 0), by_dim(wqkv[D:2 * D], 0), wqkv[2 * D:].T], axis=1),
        "woT": np.asarray(L0_attn_w_out).T,
        "gamma": np.asarray(L0_attn_gamma).reshape(KT, P).T,
        "beta": np.asarray(L0_attn_beta).reshape(KT, P).T,
        "xqT": by_dim(np.asarray(L0_xattn_Wq), 1),
        "xkT": by_dim(np.asarray(L0_xattn_Wk), 1),
        "xvT": np.asarray(L0_xattn_Wv).T,
        "w_gate": np.asarray(L0_ffn_w_gate),
        "w_up": np.asarray(L0_ffn_w_up),
        "w_down": np.asarray(L0_ffn_w_down),
    }
    nc = bacc.Bacc("TRN2", target_bir_lowering=False, num_devices=1)
    arrays, args = {}, []
    for name, a in laid.items():
        a = np.ascontiguousarray(a)
        arrays[f"in_{name}"] = a
        args.append(nc.dram_tensor(f"in_{name}", a.shape, mybir.dt.from_np(a.dtype), kind="ExternalInput").ap())
    args.append(nc.dram_tensor("out_y", [TOK, D], F32, kind="ExternalOutput").ap())
    decoder_layer(nc, *args)
    r = run_bass_kernel_spmd(nc, [arrays], core_ids=[0])
    return r.results[0]["out_y"].reshape(NB, P, D)
```

```python
from contextlib import ExitStack

import numpy as np
import concourse.bass as bass
from concourse import mybir

F32 = mybir.dt.float32
BF16 = mybir.dt.bfloat16
ALU = mybir.AluOpType
ACT = mybir.ActivationFunctionType
AX_X = mybir.AxisListType.X

P = 128
D = 256
KT = D // P
HEADS = 16
HD = D // HEADS
WINDOW = 64
LN_EPS = 1e-5
FF = 768
BLOCK = 32
QMAX = 32767.0
WQMAX = 7.0
SIG_LEVELS = 65536.0
SCALE_FLOOR = 1e-12
ROUND = 12582912.0
MASKED = -1e38
ONE_PAIR = float(np.array([0x3F803F80], np.uint32).view(np.float32)[0])

NB = 16
TOK = NB * P
CB = 4
NCH = NB // CB
CT = CB * P
HU = HEADS // 2
UPI = 8
ITERS = NB * 2 // UPI
SLOTS = UPI // 2
SPLIT = 3
COMBOS = [(0, 1), (0, 0), (0, 2), (1, 0), (1, 1), (2, 0)]
STACK = len(COMBOS) * HD
NEG = STACK
VW = HD + 1
FT = FF // P
HALF = TOK // 2
POOL_ROWS = (1, 3)

UNIT_HEADS = [[[HU * half + i for i in range(HU)] for half in range(2)],
              [[4 * (i % 4) + 2 * half + i // 4 for i in range(HU)] for half in range(2)]]


def stack_rows(side, part):
    at = [i for i, c in enumerate(COMBOS) if c[side] == part]
    step = at[1] - at[0] if len(at) > 1 else 1
    assert at == list(range(at[0], at[-1] + 1, step))
    return at[0], step, len(at)


def decoder_layer(nc, x, ctxT, wqkvT, woT, gamma, beta, xqT, xkT, xvT, w_gate, w_up, w_down, out):
    stacks = [[nc.dram_tensor(f"stack_{l}_{s}", [len(COMBOS), D, TOK], BF16, kind="Internal").ap()
               for s in range(2)] for l in range(2)]
    x_v = x.rearrange("(b p) d -> p b d", p=P)
    out_v = out.rearrange("(b p) d -> p b d", p=P)

    with ExitStack() as ctx:
        def sb(name, shape, dt=F32):
            return ctx.enter_context(nc.sbuf_tensor(name, shape, dt))

        def sem(name):
            return ctx.enter_context(nc.semaphore(name))

        resid = sb("resid", [P, NB, D])
        y = sb("y", [P, NB, D])
        w_qkv = sb("w_qkv", [P, KT, 3 * D])
        w_o = sb("w_o", [P, KT, D])
        w_x = sb("w_x", [P, 3, KT, D])
        gam = sb("gam", [P, KT])
        bet = sb("bet", [P, KT])
        w_gu = sb("w_gu", [P, 2 * FT, D])
        w_dn = sb("w_dn", [P, KT, FF])
        w_guT = sb("w_guT", [P, KT, 2 * FF])
        w_dnT = sb("w_dnT", [P, FT, D])
        x_intT = sb("x_intT", [P, KT, TOK])
        ident = sb("ident", [P, P])
        ident_b = sb("ident_b", [P, P], BF16)
        band = sb("band", [P, 4, P], BF16)
        zero = sb("zero", [P, HU])
        eps = sb("eps", [P, 1])
        rounder = sb("rounder", [P, 1])
        unrounder = sb("unrounder", [P, 1])
        stats = sb("stats", [P, NB, 6])
        mv = sb("mv", [P, NB, 2])
        sd = sb("sd", [P, NB])
        rstd = sb("rstd", [P, NB])
        nmr = sb("nmr", [P, NB])
        negm = sb("negm", [P, 4, HU])
        mparts = sb("mparts", [P, 4, SPLIT * HU], BF16)
        mrest = sb("mrest", [P, HU])
        m_T = sb("m_T", [SPLIT * HU, 4, P], BF16)
        attn = sb("attn", [P, 2, D])
        attnT = sb("attnT", [P, KT, P])
        rec = sb("rec", [P, 2, HEADS])
        o_tr = sb("o_tr", [P, 2 * P * 2])
        ablk = sb("ablk", [P, 2 * FT * 8 + KT * 24])
        wscale = sb("wscale", [P, 2 * FT * 8 + KT * 24])
        winv = sb("winv", [P, 2 * FT * 8 + KT * 24])
        tmax = sb("tmax", [P, NB])
        gmax = sb("gmax", [P, FT])
        umax = sb("umax", [P, FT])
        pmax = sb("pmax", [P, FT])
        omax = sb("omax", [P, FT])
        sc = sb("sc", [P, 32])

        arena_g = sb("arena_g", [P, FT * TOK])
        arena_u = sb("arena_u", [P, FT * TOK])
        gate = arena_g[:, :].rearrange("p (f k) -> p f k", f=FT)
        up = arena_u[:, :].rearrange("p (f k) -> p f k", f=FT)
        used = {"g": 0, "u": 0}

        def carve(which, words, dt=F32):
            a = {"g": arena_g, "u": arena_u}[which]
            at = used[which]
            used[which] = at + words
            assert at + words <= FT * TOK
            v = a[:, at:at + words]
            return v if dt == F32 else v.bitcast(dt)

        q_stk = carve("g", SLOTS * HEADS * P // 2, BF16).rearrange("p (s h k) -> p s h k", s=SLOTS, h=HEADS)
        k_stk = carve("g", SLOTS * HEADS * P // 2, BF16).rearrange("p (s h k) -> p s h k", s=SLOTS, h=HEADS)
        parts = carve("g", 4 * SPLIT * CT // 2, BF16).rearrange("p (j s k) -> p j s k", j=4, s=SPLIT)
        rest = carve("g", 2 * CT).rearrange("p (j k) -> p j k", j=2)
        v_all = carve("u", NB * HEADS * VW).rearrange("p (b h w) -> p b h w", b=NB, h=HEADS)
        v_slot = carve("u", SLOTS * HEADS * VW).rearrange("p (s h w) -> p s h w", s=SLOTS, h=HEADS)
        probT = carve("u", 2 * HU * P).rearrange("p (s h k) -> p s h k", s=2, h=HU)
        xT = carve("u", 2 * KT * CT).rearrange("p (s k t) -> p s k t", s=2, k=KT)
        cT = carve("u", 2 * KT * CT).rearrange("p (s k t) -> p s k t", s=2, k=KT)
        o_sb = carve("u", 2 * 2 * P).rearrange("p (s k) -> p s k", s=2)
        sig = y[:, :, :].rearrange("p (s b) d -> p s (b d)", s=2)

        bank = ctx.enter_context(nc.psum_tensor("bank", [P, 8, 512], F32))
        ps_s = bank[:, 0:2, :].rearrange("p b (h k) -> p (b h) k", h=4)
        ps_st = bank[:, 2:4, :].rearrange("p b (h k) -> p (b h) k", h=4)
        ps_pv = bank[:, 4, 0:2 * P]
        ps_ot = bank[:, 5, 0:2 * P]
        ps_mt = bank[:, 6, 0:P // 2].bitcast(BF16)
        ps_ap = bank[:, 7, :]

        x_landed = [sem(f"x_landed{c}") for c in range(NCH)]
        w1_landed = sem("w1_landed")
        w2_landed = sem("w2_landed")
        wf_landed = sem("wf_landed")
        ctx_landed = [sem(f"ctx_landed{i}") for i in range(2)]
        out_landed = sem("out_landed")
        consts = sem("consts")
        pool_init = sem("pool_init")
        band_half = sem("band_half")

        def layer_semaphores(l):
            names = ("xT_t", "xT_ready", "proj_done", "v_done", "v_ready", "hi_ready", "rest_ready", "mid_ready",
                     "lo_ready", "scores_done", "max_done", "mchain", "mparts_ready", "mT_done", "mT_ready",
                     "scoresT_done", "exp_done", "pv_done", "o_ready", "oT_done", "rec_ready", "norm_done",
                     "aT_done", "aT_ready", "outp_done", "resid_done", "stats_done", "mv_done",
                     "pv_zero")
            sems = {n: sem(f"l{l}_{n}") for n in names}
            sems["stored"] = [sem(f"l{l}_stored{j}") for j in range(4)]
            sems["qk_landed"] = [sem(f"l{l}_qk_landed{j}") for j in range(SLOTS)]
            sems["v_landed"] = [sem(f"l{l}_v_landed{j}") for j in range(SLOTS)]
            sems["neg_landed"] = [sem(f"l{l}_neg_landed{j}") for j in range(2)]
            return sems

        L = [layer_semaphores(l) for l in range(2)]

        bn_done = sem("bn_done")
        ln_stats = sem("ln_stats")
        ln_sd = sem("ln_sd")
        ln_link = sem("ln_link")
        ln_coef = sem("ln_coef")
        ln_apply = sem("ln_apply")
        ln_add = sem("ln_add")
        wq_link = sem("wq_link")
        wq_done = sem("wq_done")
        ones_set = sem("ones_set")
        w_t = sem("w_t")
        w_ready = sem("w_ready")
        dve_link = sem("dve_link")
        x_abs = sem("x_abs")
        red_in = sem("red_in")
        red_out = sem("red_out")
        scale_ready = sem("scale_ready")
        xq = sem("xq")
        xq_t = sem("xq_t")
        xq_ready = sem("xq_ready")
        ff_done = sem("ff_done")
        ff_evac = sem("ff_evac")
        ff_abs = sem("ff_abs")
        g_round = sem("g_round")
        g_int = sem("g_int")
        sig_done = sem("sig_done")
        sig_round = sem("sig_round")
        sig_int = sem("sig_int")
        gs_done = sem("gs_done")
        gs_abs = sem("gs_abs")
        u_round = sem("u_round")
        u_int = sem("u_int")
        gs_round = sem("gs_round")
        gs_int = sem("gs_int")
        o_done = sem("o_done")
        o_pool = sem("o_pool")
        o_abs = sem("o_abs")
        o_round = sem("o_round")
        o_int = sem("o_int")
        down_done = sem("down_done")
        y_done = sem("y_done")

        block = ctx.enter_context(nc.Block())

        def when(eng, s, value):
            if not isinstance(value, int) or value > 0:
                eng.wait_ge(s, value)

        def run_steps(eng, step, before, after):
            for u in range(-before, UPI):
                step(0, u, lambda k: k >= 0)
            with eng.Fori(1, ITERS - 1) as it:
                for u in range(UPI):
                    step(it, u, lambda k: True)
            for u in range(UPI + after):
                step(ITERS - 1, u, lambda k: k < UPI)

        def ff_pair(m):
            return (gate if m < 2 * FT else up)[:, m // 2 % FT, m % 2 * HALF:(m % 2 + 1) * HALF]

        PARTS_OF = [[0, 1, 2, 3], [2, 3, 0, 1]]

        @block.sync
        def _(sp):
            for c in range(NCH):
                sp.dma_start(resid[:, c * CB:(c + 1) * CB, :], x_v[:, c * CB:(c + 1) * CB, :]).then_inc(x_landed[c], 16)
                if c == 0:
                    sp.dma_start(w_qkv[:, :, :], wqkvT.rearrange("(k p) n -> p k n", p=P)).then_inc(w1_landed, 16)
                    sp.dma_start(gam[:, :], gamma).then_inc(w1_landed, 16)
                    sp.dma_start(bet[:, :], beta).then_inc(w1_landed, 16)
            sp.dma_start(w_o[:, :, :], woT.rearrange("(k p) n -> p k n", p=P)).then_inc(w2_landed, 16)
            for i, w in enumerate((xqT, xkT, xvT)):
                sp.dma_start(w_x[:, i, :, :], w.rearrange("(k p) n -> p k n", p=P)).then_inc(w2_landed, 16)
            sp.dma_start(w_gu[:, 0:FT, :], w_gate.rearrange("(f p) n -> p f n", p=P)).then_inc(wf_landed, 16)
            sp.dma_start(w_gu[:, FT:2 * FT, :], w_up.rearrange("(f p) n -> p f n", p=P)).then_inc(wf_landed, 16)
            sp.dma_start(w_dn[:, :, :], w_down.rearrange("(f p) n -> p f n", p=P)).then_inc(wf_landed, 16)

            def load_ctx(c):
                if c >= 2:
                    sp.wait_ge(L[1]["proj_done"], 4 * (c - 2) + 2)
                    sp.wait_ge(L[1]["v_done"], 2 * (c - 2) + 2)
                sp.dma_start(cT[:, c % 2, :, :], ctxT[:, c * CT:(c + 1) * CT].rearrange("(k p) n -> p k n", p=P))\
                  .then_inc(ctx_landed[c % 2], 16)

            load_ctx(0)
            load_ctx(1)

            def store_parts(l, c):
                s = L[l]
                for pos, j in enumerate(PARTS_OF[l]):
                    n = 4 * c + pos
                    side, t = j // 2, j % 2
                    for part, ready in enumerate((s["hi_ready"], s["mid_ready"], s["lo_ready"])):
                        sp.wait_ge(ready, n + 1)
                        a, step, k = stack_rows(side, part)
                        dst = stacks[l][side][a:a + (k - 1) * step + 1:step, t * P:(t + 1) * P, c * CT:(c + 1) * CT]
                        sp.dma_start(dst.rearrange("c f k -> f c k"),
                                     parts[:, j, part:part + 1, :].to_broadcast([P, k, CT])).then_inc(s["stored"][j], 16)

            def stack_of(l, side, at):
                return stacks[l][side][:, :, at].rearrange("c (d h) k -> (c d) h k", h=HEADS)

            def load_qk(l, b, slot):
                at = bass.ds(b * P, P)
                sp.dma_start(q_stk[0:STACK, slot, :, :], stack_of(l, 0, at)).then_inc(L[l]["qk_landed"][slot], 16)
                sp.dma_start(k_stk[0:STACK, slot, :, :], stack_of(l, 1, at)).then_inc(L[l]["qk_landed"][slot], 16)

            def load_v(l, b, slot):
                sp.dma_start(v_slot[:, slot, :, :], v_all[:, bass.ds(b, 1), :, :].rearrange("p b h w -> p (b h) w"))\
                  .then_inc(L[l]["v_landed"][slot], 16)

            def attention(l):
                s = L[l]

                def step(it, u, exists):
                    if exists(u + 2):
                        sp.wait_ge(s["mT_ready"], it * UPI + u + 3)
                        v = u + 2
                        sp.dma_start(q_stk[NEG:NEG + SPLIT, (v // 2) % SLOTS, HU * (v % 2):HU * (v % 2) + HU, :],
                                     m_T[:, v % 4, :]).then_inc(s["neg_landed"][v % 2], 16)
                    if u >= 0 and u % 2 == 1 and exists(u + UPI):
                        b = it * SLOTS + (u // 2 + SLOTS)
                        sp.wait_ge(s["scoresT_done"], it * UPI + u + 1)
                        load_qk(l, b, u // 2)
                        sp.wait_ge(s["pv_done"], it * UPI + u + 1)
                        load_v(l, b, u // 2)

                run_steps(sp, step, 3, 0)

            for l in range(2):
                s = L[l]
                for c in range(NCH):
                    store_parts(l, c)
                    if l == 1 and c + 2 < NCH:
                        load_ctx(c + 2)
                    if c == NCH - 2:
                        for j in range(4):
                            sp.wait_ge(s["stored"][j], 16 * SPLIT)
                        sp.wait_ge(s["v_ready"], 2)
                        if l == 1:
                            sp.wait_ge(L[0]["pv_done"], 2 * NB)
                        for b in range(2):
                            load_qk(l, b, b)
                            load_v(l, b, b)
                for b in range(2, SLOTS):
                    load_qk(l, b, b)
                    load_v(l, b, b)
                for j in range(4):
                    sp.wait_ge(s["stored"][j], 16 * SPLIT * NCH)
                sp.wait_ge(s["v_ready"], 2 * NCH)
                attention(l)
            for c in range(NCH):
                sp.wait_ge(y_done, CB * (c + 1))
                sp.dma_start(out_v[:, c * CB:(c + 1) * CB, :], resid[:, c * CB:(c + 1) * CB, :]).then_inc(out_landed, 16)
            sp.wait_ge(out_landed, 16 * NCH)

        @block.gpsimd
        def _(pool):
            pool.memset(ident[:, :], 0.0).then_inc(pool_init, 1)
            pool.memset(ident_b[:, :], 0.0).then_inc(pool_init, 1)
            pool.memset(band[:, :, :], 0.0).then_inc(pool_init, 1)
            pool.wait_ge(pool_init, 3)
            for m in (ident, ident_b):
                pool.affine_select(out=m[:, :], in_=m[:, :], compare_op=ALU.not_equal, fill=1.0, base=0,
                                   pattern=[[-1, P]], channel_multiplier=1).then_inc(consts, 1)
            for sign in (1, -1):
                pool.affine_select(out=band[:, :, :], in_=band[:, :, :], compare_op=ALU.is_ge, fill=MASKED,
                                   base=WINDOW // 2, pattern=[[0, 4], [sign, P]], channel_multiplier=-sign)\
                    .then_inc(band_half if sign == 1 else consts, 1)
                if sign == 1:
                    pool.wait_ge(band_half, 1)
            pool.wait_ge(consts, 5)

            def apply(rnd, c):
                src = resid if rnd % 2 == 0 else y
                k = LN_ORDER.index((rnd, c))
                pool.wait_ge(ln_coef, k + 1)
                for b in range(c * CB, (c + 1) * CB):
                    pool.tensor_scalar(y[:, b, :], src[:, b, :], rstd[:, b:b + 1], nmr[:, b:b + 1],
                                       ALU.mult, ALU.add).then_inc(ln_apply, 1)

            def add_residual(c):
                pool.wait_ge(ln_apply, CB * (APPLY_ORDER.index((0, c)) + 1))
                for b in range(c * CB, (c + 1) * CB):
                    pool.tensor_tensor(resid[:, b, :], resid[:, b, :], y[:, b, :], ALU.add).then_inc(ln_add, 1)

            def mid_parts(l, c):
                for pos, j in enumerate(PARTS_OF[l]):
                    n = 4 * c + pos
                    pool.wait_ge(L[l]["rest_ready"], n + 1)
                    if c:
                        pool.wait_ge(L[l]["stored"][j], 16 * SPLIT * c)
                    pool.tensor_scalar(parts[:, j, 1, :], rest[:, n % 2, :], 1.0, 0.0, ALU.mult, ALU.add)\
                        .then_inc(L[l]["mid_ready"], 1)

            def neg_parts(l):
                s = L[l]

                def step(it, u, exists):
                    if not exists(u + 3):
                        return
                    v = u + 3
                    n = it * UPI + v
                    m = negm[:, v % 4, :]
                    to = [mparts[:, v % 4, i * HU:(i + 1) * HU] for i in range(SPLIT)]
                    pool.wait_ge(s["max_done"], n + 1)
                    pool.tensor_tensor(to[0], m, zero[:, :], ALU.add).then_inc(s["mchain"], 1)
                    pool.wait_ge(s["mchain"], n * 3 + 1)
                    pool.tensor_tensor(mrest[:, :], m, to[0], ALU.subtract).then_inc(s["mchain"], 1)
                    pool.wait_ge(s["mchain"], n * 3 + 2)
                    pool.tensor_tensor(to[1], mrest[:, :], zero[:, :], ALU.add).then_inc(s["mchain"], 1)
                    pool.wait_ge(s["mchain"], n * 3 + 3)
                    pool.tensor_tensor(to[2], mrest[:, :], to[1], ALU.subtract).then_inc(s["mparts_ready"], 1)
                    pool.wait_ge(s["mparts_ready"], n + 1)

                run_steps(pool, step, 3, 0)

            for kind, rnd, c in POOL_PLAN:
                if kind == "apply":
                    apply(rnd, c)
                elif kind == "add":
                    add_residual(c)
                else:
                    mid_parts(0, c)
            neg_parts(0)

            for c in range(NCH):
                mid_parts(1, c)
            neg_parts(1)

            def all_max(k):
                pool.wait_ge(red_in, k + 1)
                pool.partition_all_reduce(sc[:, 2 * k + 1:2 * k + 2], sc[:, 2 * k:2 * k + 1], P,
                                          bass.bass_isa.ReduceOp.max).then_inc(red_out, 1)

            def unround(v):
                return pool.tensor_scalar(v, v, 1.0, -ROUND, ALU.mult, ALU.add)

            all_max(0)
            all_max(1)

            def gate_int(f):
                pool.wait_ge(g_round, f + 1)
                unround(gate[:, f, :]).then_inc(g_int, 1)

            def sig_integer(f):
                v = sig[:, f % 2, :]
                pool.wait_ge(sig_done, f + 1)
                pool.tensor_scalar(v, v, SIG_LEVELS, ROUND, ALU.mult, ALU.add).then_inc(sig_round, 1)
                pool.wait_ge(sig_round, f + 1)
                unround(v).then_inc(sig_int, 1)

            gate_int(0)
            for f in range(FT):
                if f + 1 < FT:
                    gate_int(f + 1)
                sig_integer(f)
            all_max(2)
            all_max(3)
            for f in range(FT):
                pool.wait_ge(gs_round, f + 1)
                unround(gate[:, f, :]).then_inc(gs_int, 1)
                if f in POOL_ROWS:
                    pool.wait_ge(u_round, f + 1)
                    unround(up[:, f, :]).then_inc(u_int, 1)
                    pool.wait_ge(gs_int, f + 1)
                    pool.wait_ge(u_int, POOL_ROWS.index(f) + 1)
                    pool.tensor_tensor(up[:, f, :], up[:, f, :], gate[:, f, :], ALU.mult).then_inc(o_pool, 1)
            all_max(4)

        @block.scalar
        def _(act):
            act.wait_ge(consts, 5)

            def sqrt_var(rnd, c):
                a, b = c * CB, (c + 1) * CB
                act.wait_ge(ln_stats, CB * (LN_ORDER.index((rnd, c)) + 1))
                act.activation(sd[:, a:b], mv[:, a:b, 1], ACT.Sqrt, bias=eps[:, 0:1]).then_inc(ln_sd, 1)

            def evac_xT(l, c):
                s = L[l]
                act.wait_ge(s["xT_t"], c + 1)
                if c >= 2:
                    act.wait_ge(s["proj_done"], 4 * (c - 1))
                    act.wait_ge(s["v_done"], 2 * (c - 1))
                for k in range(KT):
                    if l == 0:
                        act.activation(xT[:, c % 2, k, :], bank[:, k, :], ACT.Identity, scale=gam[:, k:k + 1],
                                       bias=bet[:, k:k + 1]).then_inc(s["xT_ready"], 1)
                    else:
                        act.activation(xT[:, c % 2, k, :], bank[:, k, :], ACT.Copy).then_inc(s["xT_ready"], 1)

            def hi_parts(l, c, which):
                s = L[l]
                for pos, j in enumerate(PARTS_OF[l]):
                    if pos in which:
                        n = 4 * c + pos
                        act.wait_ge(s["proj_done"], n + 1)
                        if c:
                            act.wait_ge(s["stored"][j], 16 * SPLIT * c)
                        act.activation(parts[:, j, 0, :], bank[:, 2 + j, :], ACT.Copy).then_inc(s["hi_ready"], 1)

            def evac_v(l, c):
                s = L[l]
                for i in range(2):
                    b = c * CB + 2 * i
                    act.wait_ge(s["v_done"], 2 * c + i + 1)
                    act.activation(v_all[:, b:b + 2, :, 0:HD],
                                   bank[:, 6 + i, :].rearrange("p (b h w) -> p b h w", b=2, h=HEADS),
                                   ACT.Copy).then_inc(s["v_ready"], 1)

            def attention(l):
                s = L[l]

                def step(it, u, exists):
                    n = it * UPI + u
                    if u >= 0 and exists(u):
                        act.wait_ge(s["scoresT_done"], n + 1)
                        if exists(u - 2):
                            act.wait_ge(s["pv_done"], n - 1)
                        act.activation(probT[:, u % 2, :, :], ps_st, ACT.Exp, scale=HD ** -0.5)\
                            .then_inc(s["exp_done"], 1)
                    if l == 0 and exists(u - 1):
                        act.wait_ge(s["pv_done"], n)
                        if exists(u - 3):
                            act.wait_ge(s["oT_done"], n - 2)
                        act.activation(o_sb[:, (u - 1) % 2, :], ps_pv, ACT.Copy).then_inc(s["o_ready"], 1)
                    if exists(u + 2):
                        v = u + 2
                        act.wait_ge(s["mT_done"], n + 3)
                        act.activation(m_T[:, v % 4, :], ps_mt[0:SPLIT * HU, :], ACT.Copy).then_inc(s["mT_ready"], 1)
                    if l == 0 and u % 2 == 0 and exists(u - 4):
                        act.wait_ge(s["aT_done"], it * SLOTS + (u - 4) // 2 + 1)
                        act.activation(attnT[:, :, :], ps_ap[:, 0:D].rearrange("p (k t) -> p k t", k=KT), ACT.Copy)\
                            .then_inc(s["aT_ready"], 1)

                run_steps(act, step, 3, 5)

            act.wait_ge(w1_landed, 48)
            for kind, *a in ACT_PLAN:
                {"sqrt": sqrt_var, "xT": evac_xT, "v": evac_v, "hi": lambda l, c: hi_parts(l, c, range(4))}[kind](*a)
            attention(0)
            act.wait_ge(L[0]["mv_done"], NB)
            act.activation(sd[:, :], mv[:, :, 1], ACT.Sqrt, bias=eps[:, 0:1]).then_inc(ln_sd, 1)
            for c in range(NCH):
                hi_parts(1, c, (0, 1))
                evac_v(1, c)
                evac_xT(1, c)
                hi_parts(1, c, (2, 3))
            attention(1)
            act.wait_ge(L[1]["mv_done"], NB)
            act.activation(sd[:, :], mv[:, :, 1], ACT.Sqrt, bias=eps[:, 0:1]).then_inc(ln_sd, 1)
            for i in range(9):
                act.wait_ge(w_t, i + 1)
                if i < 6:
                    k, g = i // 3, i % 3
                    dst = w_guT[:, k, g * 512:(g + 1) * 512]
                else:
                    dst = w_dnT[:, 2 * (i - 6):2 * (i - 6) + 2, :].rearrange("p f n -> p (f n)")
                act.activation(dst, bank[:, i % 8, :], ACT.Copy).then_inc(w_ready, 1)
            for c in range(NCH):
                for k in range(KT):
                    n = c * KT + k
                    act.wait_ge(xq_t, n + 1)
                    act.activation(x_intT[:, k, c * CT:(c + 1) * CT], bank[:, (n + 1) % 8, :], ACT.Identity,
                                   bias=unrounder[:, 0:1]).then_inc(xq_ready, 1)

            def evac_ff(m):
                act.wait_ge(ff_done, 2 * m + 2)
                act.activation(ff_pair(m), bank[:, 2 * m % 8:2 * m % 8 + 2, :].rearrange("p b k -> p (b k)"), ACT.Copy)\
                   .then_inc(ff_evac, 1)

            def round_gate(f):
                if f == 0:
                    act.wait_ge(scale_ready, 2)
                act.activation(gate[:, f, :], gate[:, f, :], ACT.Identity, scale=sc[:, 13:14], bias=rounder[:, 0:1])\
                    .then_inc(g_round, 1)

            def sigmoid(f):
                act.wait_ge(g_int, f + 1)
                if f >= 2:
                    act.wait_ge(gs_done, f - 1)
                act.activation(sig[:, f % 2, :], gate[:, f, :], ACT.Sigmoid, scale=sc[:, 12:13]).then_inc(sig_done, 1)

            for m in range(2 * FT):
                evac_ff(m)
            for kind, i in ACT_FF_PLAN:
                {"evac": evac_ff, "round": round_gate, "sigmoid": sigmoid}[kind](i)
            for f in range(FT):
                if f == 0:
                    act.wait_ge(scale_ready, 3)
                act.activation(gate[:, f, :], gate[:, f, :], ACT.Identity, scale=sc[:, 15:16], bias=rounder[:, 0:1])\
                    .then_inc(gs_round, 1)
                if f == 0:
                    act.wait_ge(scale_ready, 4)
                act.activation(up[:, f, :], up[:, f, :], ACT.Identity, scale=sc[:, 17:18], bias=rounder[:, 0:1])\
                    .then_inc(u_round, 1)
            act.wait_ge(scale_ready, 5)
            for b in range(NB):
                ob = up[:, :, b * P:(b + 1) * P]
                act.activation(ob, ob, ACT.Identity, scale=sc[:, 19:20], bias=rounder[:, 0:1]).then_inc(o_round, 1)

        @block.tensor
        def _(pe):
            pe.wait_ge(consts, 5)

            def transpose_x(l, c):
                s = L[l]
                if l == 0:
                    pe.wait_ge(ln_apply, CB * (APPLY_ORDER.index((1, c)) + 1))
                else:
                    pe.wait_ge(ln_apply, CB * (2 * NCH + c + 1))
                when(pe, s["xT_ready"], KT * c)
                for k in range(KT):
                    for i in range(CB):
                        ins = pe.transpose(bank[:, k, i * P:(i + 1) * P], y[:, c * CB + i, k * P:(k + 1) * P], ident[:, :])
                ins.then_inc(s["xT_t"], 1)

            def project(l, c, which):
                s = L[l]
                for pos, j in enumerate(PARTS_OF[l]):
                    if pos not in which:
                        continue
                    n = 4 * c + pos
                    if c:
                        pe.wait_ge(s["rest_ready"], n - 3)
                    if l == 1 and j >= 2:
                        pe.wait_ge(ctx_landed[c % 2], 16 * (c // 2 + 1))
                        src = cT
                    else:
                        pe.wait_ge(s["xT_ready"], KT * (c + 1))
                        src = xT
                    for k in range(KT):
                        w = (w_qkv[:, k, j * P:(j + 1) * P] if l == 0 else
                             w_x[:, j // 2, k, (j % 2) * P:(j % 2 + 1) * P])
                        ins = pe.matmul(bank[:, 2 + j, :], w, src[:, c % 2, k, :], start=(k == 0), stop=(k == KT - 1))
                    ins.then_inc(s["proj_done"], 1)

            def values(l, c):
                s = L[l]
                src = xT if l == 0 else cT
                for i in range(CB):
                    if i % 2 == 0 and c:
                        pe.wait_ge(s["v_ready"], 2 * (c - 1) + i // 2 + 1)
                    for k in range(KT):
                        w = w_qkv[:, k, 2 * D:3 * D] if l == 0 else w_x[:, 2, k, :]
                        ins = pe.matmul(bank[:, 6 + i // 2, (i % 2) * D:(i % 2 + 1) * D],
                                        src[:, c % 2, k, i * P:(i + 1) * P], w, start=(k == 0), stop=(k == KT - 1))
                    if i % 2:
                        ins.then_inc(s["v_done"], 1)

            def attention(l):
                s = L[l]
                pe.wait_ge(s["xT_ready"], KT * NCH)
                pe.wait_ge(s["rest_ready"], 4 * NCH)
                pe.wait_ge(s["v_ready"], 2 * NCH)
                pe.wait_ge(s["pv_zero"], l + 1)
                pe.wait_ge(ones_set, 1)

                def scores(it, u):
                    slot = (u // 2) % SLOTS
                    if u % 2 == 0:
                        pe.wait_ge(s["qk_landed"][slot], (it + u // UPI) * 32 + 32)
                    if not (isinstance(it, int) and it * UPI + u == 0):
                        pe.wait_ge(s["max_done"], it * UPI + u)
                    if l == 0:
                        for g in range(2):
                            pe.matmul(bank[:, g, :], ident_b[:, :], band[:, :, :].rearrange("p h k -> p (h k)"),
                                      start=True, stop=False, skip_group_check=True)
                    for i in range(HU):
                        h = HU * (u % 2) + i
                        ins = pe.matmul(ps_s[:, i, :], q_stk[0:STACK, slot, h, :], k_stk[0:STACK, slot, h, :],
                                        start=(l == 1), stop=True, skip_group_check=True)
                    ins.then_inc(s["scores_done"], 1)

                def scores_T(it, u):
                    slot = (u // 2) % SLOTS
                    pe.wait_ge(s["neg_landed"][u % 2], it * (16 * UPI // 2) + 16 * (u // 2 + 1))
                    if not (isinstance(it, int) and it * UPI + u == 0):
                        pe.wait_ge(s["exp_done"], it * UPI + u)
                    if l == 0:
                        for g in range(2):
                            pe.matmul(bank[:, 2 + g, :], ident_b[:, :], band[:, :, :].rearrange("p h k -> p (h k)"),
                                      start=True, stop=False, skip_group_check=True)
                    for i in range(HU):
                        h = HU * (u % 2) + i
                        ins = pe.matmul(ps_st[:, i, :], k_stk[0:NEG + SPLIT, slot, h, :], q_stk[0:NEG + SPLIT, slot, h, :],
                                        start=(l == 1), stop=True, skip_group_check=True)
                    ins.then_inc(s["scoresT_done"], 1)

                def weighted(it, u, has_before):
                    slot = (u // 2) % SLOTS
                    if u % 2 == 0:
                        pe.wait_ge(s["v_landed"][slot], (it + u // UPI) * 16 + 16)
                    pe.wait_ge(s["exp_done"], it * UPI + u + 1)
                    if has_before:
                        if l == 0:
                            pe.wait_ge(s["o_ready"], it * UPI + u)
                        elif u % 2 == 0:
                            pe.wait_ge(s["o_ready"], it * SLOTS + u // 2 - 1)
                    for i in range(HU):
                        h = UNIT_HEADS[l][u % 2][i]
                        r = 32 * (i % 4)
                        at = i // 4 * P + (l * (u % 2) * 2 * P)
                        out_bank = 4 + l * (u // 2 % 2)
                        ins = pe.matmul(bank[r:r + VW, out_bank, at:at + P], v_slot[:, slot, h, :],
                                        probT[:, u % 2, i, :], start=True, stop=True, skip_group_check=True)
                    ins.then_inc(s["pv_done"], 1)

                def step(it, u, exists):
                    n = it * UPI + u
                    if exists(u + 3):
                        scores(it, u + 3)
                    if u >= 0 and exists(u):
                        scores_T(it, u)
                    if exists(u - 1):
                        weighted(it, u - 1, exists(u - 2) if l == 0 else exists(u - 5))
                    if exists(u + 2):
                        v = u + 2
                        pe.wait_ge(s["mparts_ready"], n + 3)
                        if exists(u + 1):
                            pe.wait_ge(s["mT_ready"], n + 2)
                        pe.transpose(ps_mt[0:SPLIT * HU, :], mparts[:, v % 4, :], ident_b[:, :]).then_inc(s["mT_done"], 1)
                    if l == 0 and exists(u - 2):
                        v = u - 2
                        pe.wait_ge(s["o_ready"], n - 1)
                        if exists(u - 3):
                            pe.wait_ge(s["norm_done"], n - 2)
                        for g in range(2):
                            ins = pe.transpose(ps_ot[:, g * P:(g + 1) * P], o_sb[:, v % 2, g * P:(g + 1) * P], ident[:, :])
                        ins.then_inc(s["oT_done"], 1)
                    if l == 0 and u % 2 == 0 and exists(u - 4):
                        v = u - 4
                        nb = it * SLOTS + v // 2
                        pe.wait_ge(s["norm_done"], it * UPI + v + 2)
                        if exists(v - 2):
                            pe.wait_ge(s["resid_done"], nb)
                        for k in range(KT):
                            ins = pe.transpose(ps_ap[:, k * P:(k + 1) * P], attn[:, (v // 2) % 2, k * P:(k + 1) * P], ident[:, :])
                        ins.then_inc(s["aT_done"], 1)
                    if l == 0 and u % 2 == 1 and exists(u - 5):
                        nb = it * SLOTS + (u - 5) // 2
                        pe.wait_ge(s["aT_ready"], nb + 1)
                        for k in range(KT):
                            ins = pe.matmul(ps_ap[:, 0:D], attnT[:, k, :], w_o[:, k, :], start=(k == 0), stop=(k == KT - 1))
                        ins.then_inc(s["outp_done"], 1)

                run_steps(pe, step, 3, 6)

            pe.wait_ge(w1_landed, 48)
            transpose_x(0, 0)
            for c in range(NCH):
                project(0, c, range(4))
                if c + 1 < NCH:
                    transpose_x(0, c + 1)
                values(0, c)
            pe.wait_ge(w2_landed, 64)
            attention(0)
            pe.wait_ge(L[0]["max_done"], 2 * NB)
            pe.wait_ge(L[0]["exp_done"], 2 * NB)
            pe.wait_ge(L[0]["norm_done"], 2 * NB)
            pe.wait_ge(L[0]["resid_done"], NB)
            for c in range(NCH):
                project(1, c, (0, 1))
                values(1, c)
                transpose_x(1, c)
                project(1, c, (2, 3))
            attention(1)
            pe.wait_ge(L[1]["resid_done"], NB)
            pe.wait_ge(wq_done, 9)
            for i in range(9):
                if i == 8:
                    pe.wait_ge(w_ready, 1)
                for j in range(4):
                    if i < 6:
                        k, f = i // 3, (i % 3) * 4 + j
                        src = w_gu[:, f, k * P:(k + 1) * P]
                    else:
                        f, k = 2 * (i - 6) + j // 2, j % 2
                        src = w_dn[:, k, f * P:(f + 1) * P]
                    ins = pe.transpose(bank[:, i % 8, j * P:(j + 1) * P], src, ident[:, :])
                ins.then_inc(w_t, 1)
            for c in range(NCH):
                pe.wait_ge(xq, c + 1)
                for k in range(KT):
                    n = c * KT + k
                    pe.wait_ge(w_ready, min(9, n + 2))
                    for i in range(CB):
                        ins = pe.transpose(bank[:, (n + 1) % 8, i * P:(i + 1) * P], y[:, c * CB + i, k * P:(k + 1) * P], ident[:, :])
                    ins.then_inc(xq_t, 1)
            pe.wait_ge(w_ready, 9)
            pe.wait_ge(xq_ready, KT * NCH)
            for n in range(2 * FT * NCH):
                f, c = n // NCH, n % NCH
                if n >= 8 and n % 2 == 0:
                    pe.wait_ge(ff_evac, n // 2 - 3)
                for k in range(KT):
                    ins = pe.matmul(bank[:, n % 8, :], w_guT[:, k, f * P:(f + 1) * P],
                                    x_intT[:, k, c * CT:(c + 1) * CT], start=(k == 0), stop=(k == KT - 1))
                ins.then_inc(ff_done, 1)
            pe.wait_ge(ff_evac, 4 * FT)
            for b in range(NB):
                pe.wait_ge(o_int, b + 1)
                if b >= 8:
                    pe.wait_ge(y_done, b - 7)
                for f in range(FT):
                    ins = pe.matmul(bank[:, b % 8, 0:D], up[:, f, b * P:(b + 1) * P], w_dnT[:, f, :],
                                    start=(f == 0), stop=(f == FT - 1))
                ins.then_inc(down_done, 1)

        @block.vector
        def _(dve):
            dve.memset(eps[:, :], LN_EPS).then_inc(dve_link, 1)
            dve.memset(rounder[:, :], ROUND).then_inc(dve_link, 1)
            dve.memset(unrounder[:, :], -ROUND).then_inc(dve_link, 1)
            dve.memset(v_all[:, :, :, HD:VW], 1.0).then_inc(consts, 1)
            dve.memset(zero[:, :], 0.0).then_inc(consts, 1)
            dve.wait_ge(dve_link, 3)
            chain = [3]

            def link(ins):
                chain[0] += 1
                ins.then_inc(dve_link, 1)
                dve.wait_ge(dve_link, chain[0])

            def norm_stats(rnd, c):
                src = resid if rnd == 0 else y
                k = LN_ORDER.index((rnd, c))
                if rnd == 0:
                    dve.wait_ge(x_landed[c], 16)
                else:
                    dve.wait_ge(ln_apply, CB * (APPLY_ORDER.index((0, c)) + 1))
                    dve.wait_ge(ln_coef, LN_ORDER.index((0, c)) + 1)
                for b in range(c * CB, (c + 1) * CB):
                    dve.bn_stats(stats[:, b, :], src[:, b, :]).then_inc(bn_done, 1)
                dve.wait_ge(bn_done, CB * (k + 1))
                for b in range(c * CB, (c + 1) * CB):
                    dve.bn_aggr(mv[:, b, :], stats[:, b, :]).then_inc(ln_stats, 1)

            def norm_coef(k, a, b):
                dve.wait_ge(ln_sd, k + 1)
                dve.reciprocal(rstd[:, a:b], sd[:, a:b]).then_inc(ln_link, 1)
                dve.wait_ge(ln_link, k + 1)
                dve.scalar_tensor_tensor(out=nmr[:, a:b], in0=mv[:, a:b, 0], scalar=-1.0, in1=rstd[:, a:b],
                                         op0=ALU.mult, op1=ALU.mult).then_inc(ln_coef, 1)

            def low_part(l, n):
                s = L[l]
                j = PARTS_OF[l][n % 4]
                dve.wait_ge(s["mid_ready"], n + 1)
                dve.tensor_tensor(parts[:, j, 2, :], rest[:, n % 2, :], parts[:, j, 1, :], ALU.subtract)\
                   .then_inc(s["lo_ready"], 1)

            def split(l, c, which):
                s = L[l]
                for pos, j in enumerate(PARTS_OF[l]):
                    if pos not in which:
                        continue
                    n = 4 * c + pos
                    dve.wait_ge(s["hi_ready"], n + 1)
                    if n >= 2:
                        dve.wait_ge(s["lo_ready"], n - 1)
                    dve.tensor_tensor(rest[:, n % 2, :], bank[:, 2 + j, :], parts[:, j, 0, :], ALU.subtract)\
                       .then_inc(s["rest_ready"], 1)
                    if n:
                        low_part(l, n - 1)

            def residual_stats(s, nb):
                dve.wait_ge(s["resid_done"], nb + 1)
                dve.bn_stats(stats[:, bass.ds(nb, 1), :], resid[:, bass.ds(nb, 1), :]).then_inc(s["stats_done"], 1)

            def all_moments(s):
                dve.wait_ge(s["stats_done"], NB)
                for b in range(NB):
                    dve.bn_aggr(mv[:, b, :], stats[:, b, :]).then_inc(s["mv_done"], 1)

            def attention(l):
                s = L[l]
                dve.wait_ge(s["rest_ready"], 4 * NCH)
                dve.wait_ge(s["proj_done"], 4 * NCH)
                for i in range(l + 1):
                    dve.memset(bank[:, 4 + i, :], 0.0).then_inc(s["pv_zero"], 1)

                def step(it, u, exists):
                    n = it * UPI + u
                    if exists(u + 3):
                        v = u + 3
                        dve.wait_ge(s["scores_done"], n + 4)
                        dve.tensor_reduce(negm[:, v % 4, :], ps_s, AX_X, ALU.max, negate=True).then_inc(s["max_done"], 1)
                    if l == 0 and exists(u - 2):
                        v = u - 2
                        hs = HU * (v % 2)
                        dve.wait_ge(s["oT_done"], n - 1)
                        ot = ps_ot.rearrange("p (h w) -> p h w", h=HU)
                        dve.reciprocal(rec[:, v % 2, 0:HU], ot[:, :, HD]).then_inc(s["rec_ready"], 1)
                        dve.wait_ge(s["rec_ready"], n - 1)
                        if exists(v - 4):
                            dve.wait_ge(s["aT_done"], it * SLOTS + v // 2 - 1)
                        dst = attn[:, (v // 2) % 2, hs * HD:(hs + HU) * HD]
                        dve.tensor_tensor(dst.rearrange("p (h w) -> p h w", h=HU), ot[:, :, 0:HD],
                                          rec[:, v % 2, 0:HU].unsqueeze(2).to_broadcast([P, HU, HD]), ALU.mult)\
                           .then_inc(s["norm_done"], 1)
                    if l == 1 and u % 2 == 0 and exists(u - 1):
                        v = u - 2
                        nb = it * SLOTS + v // 2
                        dve.wait_ge(s["pv_done"], n)
                        src = bank[:, 4 + v // 2 % 2, :].rearrange("p (g j i) -> p i g j", g=4, j=HU)
                        dve.transpose(o_tr[:, :], src).then_inc(s["o_ready"], 1)
                        dve.wait_ge(s["o_ready"], nb + 1)
                        ot = o_tr[:, :].rearrange("p (i w) -> p i w", w=32)
                        dve.reciprocal(rec[:, 0, :], ot[:, :, HD]).then_inc(s["rec_ready"], 1)
                        dve.wait_ge(s["rec_ready"], nb + 1)
                        dst = attn[:, 0, :]
                        dve.tensor_tensor(dst.rearrange("p (i w) -> p i w", w=HD), ot[:, :, 0:HD],
                                          rec[:, 0, :].unsqueeze(2).to_broadcast([P, HEADS, HD]), ALU.mult)\
                           .then_inc(s["norm_done"], 1)
                        dve.wait_ge(s["norm_done"], nb + 1)
                        r = resid[:, bass.ds(nb, 1), :].rearrange("p b w -> p (b w)")
                        dve.tensor_tensor(r, r, dst, ALU.add).then_inc(s["resid_done"], 1)
                        residual_stats(s, nb)
                    if l == 0 and u % 2 == 1 and exists(u - 5):
                        nb = it * SLOTS + (u - 5) // 2
                        dve.wait_ge(s["outp_done"], nb + 1)
                        r = resid[:, bass.ds(nb, 1), :].rearrange("p b w -> p (b w)")
                        dve.tensor_tensor(r, ps_ap[:, 0:D], r, ALU.add).then_inc(s["resid_done"], 1)
                        residual_stats(s, nb)

                run_steps(dve, step, 3, 6)

            W_PIECES = [(w_gu[:, 0:FT, :], 0), (w_gu[:, FT:2 * FT, :], FT * 8), (w_dn[:, :, :], 2 * FT * 8)]

            def weight_scales(i):
                w, at = W_PIECES[i]
                n = w.shape[1] * w.shape[2] // BLOCK
                if i == 0:
                    dve.wait_ge(wf_landed, 48)
                dve.tensor_reduce(ablk[:, at:at + n], w.rearrange("p f (g e) -> p (f g) e", e=BLOCK), AX_X,
                                  ALU.max, apply_absolute_value=True).then_inc(wq_link, 1)
                dve.wait_ge(wq_link, 3 * i + 1)
                dve.tensor_scalar(wscale[:, at:at + n], ablk[:, at:at + n], 1.0 / WQMAX, SCALE_FLOOR, ALU.mult, ALU.max)\
                   .then_inc(wq_link, 1)
                dve.wait_ge(wq_link, 3 * i + 2)
                dve.reciprocal(winv[:, at:at + n], wscale[:, at:at + n]).then_inc(wq_link, 1)

            def quantise_weights(i):
                w, at = W_PIECES[i]
                n = w.shape[1] * w.shape[2] // BLOCK
                wv = w.rearrange("p f (g e) -> p (f g) e", e=BLOCK)
                dve.wait_ge(wq_link, 3 * i + 3)
                dve.tensor_tensor(wv, wv, winv[:, at:at + n].unsqueeze(2).to_broadcast([P, n, BLOCK]), ALU.mult)\
                   .then_inc(wq_done, 1)
                dve.wait_ge(wq_done, 3 * i + 1)
                dve.tensor_scalar(wv, wv, ROUND, -ROUND, ALU.add, ALU.add).then_inc(wq_done, 1)
                dve.wait_ge(wq_done, 3 * i + 2)
                dve.tensor_tensor(wv, wv, wscale[:, at:at + n].unsqueeze(2).to_broadcast([P, n, BLOCK]), ALU.mult)\
                   .then_inc(wq_done, 1)

            for kind, *a in DVE_PLAN:
                if kind == "stats":
                    norm_stats(*a)
                elif kind == "coef":
                    rnd, c = a
                    norm_coef(LN_ORDER.index((rnd, c)), c * CB, (c + 1) * CB)
                elif kind == "wscale":
                    weight_scales(*a)
                else:
                    split(0, a[0], range(4))
            low_part(0, 4 * NCH - 1)
            dve.memset(k_stk[NEG:NEG + SPLIT, :, :, :].bitcast(F32), ONE_PAIR).then_inc(ones_set, 1)
            dve.wait_ge(ln_add, NB)
            attention(0)
            all_moments(L[0])
            norm_coef(2 * NCH, 0, NB)
            dve.wait_ge(ln_coef, 2 * NCH + 1)

            def apply(c):
                for b in range(c * CB, (c + 1) * CB):
                    dve.tensor_scalar(y[:, b, :], resid[:, b, :], rstd[:, b:b + 1], nmr[:, b:b + 1], ALU.mult, ALU.add)\
                       .then_inc(ln_apply, 1)

            apply(0)
            for c in range(NCH):
                split(1, c, (0, 1))
                if c + 1 < NCH:
                    apply(c + 1)
                    quantise_weights(c)
                split(1, c, (2, 3))
            low_part(1, 4 * NCH - 1)
            attention(1)
            all_moments(L[1])
            norm_coef(2 * NCH + 1, 0, NB)
            dve.wait_ge(ln_coef, 2 * NCH + 2)
            for b in range(NB):
                dve.tensor_scalar(y[:, b, :], resid[:, b, :], rstd[:, b:b + 1], nmr[:, b:b + 1], ALU.mult, ALU.add)\
                   .then_inc(ln_apply, 1)
            dve.wait_ge(ln_apply, CB * 4 * NCH)
            link(dve.tensor_reduce(tmax[:, :], y[:, :, :], AX_X, ALU.max, apply_absolute_value=True))

            def quant_scale(k, cells, prefactor):
                dve.tensor_reduce(sc[:, 2 * k:2 * k + 1], cells, AX_X, ALU.max).then_inc(red_in, 1)
                dve.wait_ge(red_out, k + 1)
                s_, m_ = sc[:, 10 + 2 * k:11 + 2 * k], sc[:, 11 + 2 * k:12 + 2 * k]
                if prefactor is None:
                    link(dve.tensor_scalar(s_, sc[:, 2 * k + 1:2 * k + 2], 1.0 / QMAX, SCALE_FLOOR, ALU.mult, ALU.max))
                    dve.reciprocal(m_, s_).then_inc(scale_ready, 1)
                else:
                    link(dve.tensor_scalar(sc[:, 24:25], sc[:, 2 * k + 1:2 * k + 2], prefactor, 1.0 / QMAX, ALU.mult, ALU.mult))
                    link(dve.tensor_scalar(s_, sc[:, 24:25], SCALE_FLOOR, None, ALU.max))
                    link(dve.reciprocal(sc[:, 25:26], s_))
                    dve.tensor_scalar(m_, sc[:, 25:26], prefactor, None, ALU.mult).then_inc(scale_ready, 1)
                dve.wait_ge(scale_ready, k + 1)

            quant_scale(0, tmax[:, :], None)
            for c in range(NCH):
                yc = y[:, c * CB:(c + 1) * CB, :]
                dve.tensor_scalar(yc, yc, sc[:, 11:12], ROUND, ALU.mult, ALU.add).then_inc(xq, 1)

            def row_max(cells, v, f, done):
                dve.tensor_reduce(cells[:, f:f + 1], v[:, f, :], AX_X, ALU.max, apply_absolute_value=True).then_inc(done, 1)

            def row_max_ff(r):
                dve.wait_ge(ff_evac, 2 * r + 2)
                row_max(gmax if r < FT else umax, gate if r < FT else up, r % FT, ff_abs)

            for r in range(FT):
                row_max_ff(r)
            dve.wait_ge(ff_abs, FT)
            quant_scale(1, gmax[:, :], sc[:, 10:11])
            link(dve.tensor_scalar(sc[:, 26:27], sc[:, 12:13], 1.0 / SIG_LEVELS, None, ALU.mult))
            for f in range(FT):
                dve.wait_ge(sig_int, f + 1)
                dve.scalar_tensor_tensor(out=gate[:, f, :], in0=sig[:, f % 2, :], scalar=SIG_LEVELS - 1, in1=gate[:, f, :],
                                         op0=ALU.min, op1=ALU.mult).then_inc(gs_done, 1)
                dve.wait_ge(gs_done, f + 1)
                row_max(pmax, gate, f, gs_abs)
                if f:
                    row_max_ff(FT + f - 1)
            dve.wait_ge(gs_abs, FT)
            quant_scale(2, pmax[:, :], sc[:, 26:27])
            row_max_ff(2 * FT - 1)
            dve.wait_ge(ff_abs, 2 * FT)
            quant_scale(3, umax[:, :], sc[:, 10:11])
            link(dve.tensor_scalar(sc[:, 27:28], sc[:, 14:15], sc[:, 16:17], None, ALU.mult))
            own = [f for f in range(FT) if f not in POOL_ROWS]
            for i, f in enumerate(own):
                dve.wait_ge(u_round, f + 1)
                dve.wait_ge(gs_int, f + 1)
                dve.scalar_tensor_tensor(out=up[:, f, :], in0=up[:, f, :], scalar=-ROUND, in1=gate[:, f, :],
                                         op0=ALU.add, op1=ALU.mult).then_inc(o_done, 1)
                dve.wait_ge(o_done, i + 1)
                row_max(omax, up, f, o_abs)
                if i >= 2 and i - 2 < len(POOL_ROWS):
                    dve.wait_ge(o_pool, i - 1)
                    row_max(omax, up, POOL_ROWS[i - 2], o_abs)
            dve.wait_ge(o_abs, FT)
            quant_scale(4, omax[:, :], sc[:, 27:28])

            def final(b):
                dve.wait_ge(down_done, b + 1)
                dve.scalar_tensor_tensor(out=resid[:, b, :], in0=bank[:, b % 8, 0:D], scalar=sc[:, 18:19],
                                         in1=resid[:, b, :], op0=ALU.mult, op1=ALU.add).then_inc(y_done, 1)

            for b in range(NB):
                ob = up[:, :, b * P:(b + 1) * P]
                dve.wait_ge(o_round, b + 1)
                dve.tensor_scalar(ob, ob, -ROUND, None, ALU.add).then_inc(o_int, 1)
                if b >= 3:
                    final(b - 3)
            for b in range(NB - 3, NB):
                final(b)


LN_ORDER = [(0, 0), (0, 1), (0, 2), (1, 0), (0, 3), (1, 1), (1, 2), (1, 3)]
DVE_PLAN = [("stats", 0, 0), ("stats", 0, 1), ("coef", 0, 0), ("stats", 0, 2), ("coef", 0, 1), ("stats", 1, 0),
            ("coef", 0, 2), ("stats", 0, 3), ("coef", 1, 0), ("stats", 1, 1), ("coef", 0, 3), ("coef", 1, 1),
            ("split", 0), ("stats", 1, 2), ("coef", 1, 2), ("wscale", 0), ("split", 1), ("stats", 1, 3), ("coef", 1, 3),
            ("wscale", 1), ("split", 2), ("wscale", 2), ("split", 3)]
POOL_PLAN = [("apply", 0, 0), ("apply", 0, 1), ("add", 0, 0), ("apply", 0, 2), ("apply", 1, 0), ("add", 0, 1),
             ("apply", 0, 3), ("apply", 1, 1), ("add", 0, 2), ("add", 0, 3), ("mid", 0, 0), ("apply", 1, 2),
             ("mid", 0, 1), ("apply", 1, 3), ("mid", 0, 2), ("mid", 0, 3)]
APPLY_ORDER = [(r, c) for k, r, c in POOL_PLAN if k == "apply"]
ACT_PLAN = [("sqrt", 0, 0), ("sqrt", 0, 1), ("sqrt", 0, 2), ("sqrt", 1, 0), ("sqrt", 0, 3), ("sqrt", 1, 1),
            ("xT", 0, 0), ("hi", 0, 0), ("xT", 0, 1), ("v", 0, 0), ("sqrt", 1, 2), ("hi", 0, 1), ("xT", 0, 2),
            ("v", 0, 1), ("sqrt", 1, 3), ("hi", 0, 2), ("xT", 0, 3), ("v", 0, 2), ("hi", 0, 3), ("v", 0, 3)]
ACT_FF_PLAN = [("evac", 12), ("round", 0), ("evac", 13), ("round", 1), ("sigmoid", 0), ("evac", 14), ("round", 2),
               ("sigmoid", 1), ("evac", 15), ("evac", 16), ("round", 3), ("sigmoid", 2), ("evac", 17), ("round", 4),
               ("sigmoid", 3), ("evac", 18), ("evac", 19), ("round", 5), ("sigmoid", 4), ("evac", 20), ("sigmoid", 5),
               ("evac", 21), ("evac", 22), ("evac", 23)]


def by_dim(w, layer):
    heads = [h for half in UNIT_HEADS[layer] for h in half]
    return w.reshape(HEADS, HD, D)[heads].transpose(2, 1, 0).reshape(D, D)


def kernel(x, ctx_1024, L0_attn_w_qkv, L0_attn_w_out, L0_attn_gamma, L0_attn_beta, L0_xattn_Wq, L0_xattn_Wk,
           L0_xattn_Wv, L0_ffn_w_gate, L0_ffn_w_up, L0_ffn_w_down):
    import concourse.bacc as bacc
    from concourse.bass_utils import run_bass_kernel_spmd

    wqkv = np.asarray(L0_attn_w_qkv)
    laid = {
        "x": np.asarray(x).reshape(TOK, D),
        "ctxT": np.asarray(ctx_1024).reshape(TOK, D).T,
        "wqkvT": np.concatenate([by_dim(wqkv[0:D], 0), by_dim(wqkv[D:2 * D], 0), wqkv[2 * D:].T], axis=1),
        "woT": np.asarray(L0_attn_w_out).T,
        "gamma": np.asarray(L0_attn_gamma).reshape(KT, P).T,
        "beta": np.asarray(L0_attn_beta).reshape(KT, P).T,
        "xqT": by_dim(np.asarray(L0_xattn_Wq), 1),
        "xkT": by_dim(np.asarray(L0_xattn_Wk), 1),
        "xvT": np.asarray(L0_xattn_Wv).T,
        "w_gate": np.asarray(L0_ffn_w_gate),
        "w_up": np.asarray(L0_ffn_w_up),
        "w_down": np.asarray(L0_ffn_w_down),
    }
    nc = bacc.Bacc("TRN2", target_bir_lowering=False, num_devices=1)
    arrays, args = {}, []
    for name, a in laid.items():
        a = np.ascontiguousarray(a)
        arrays[f"in_{name}"] = a
        args.append(nc.dram_tensor(f"in_{name}", a.shape, mybir.dt.from_np(a.dtype), kind="ExternalInput").ap())
    args.append(nc.dram_tensor("out_y", [TOK, D], F32, kind="ExternalOutput").ap())
    decoder_layer(nc, *args)
    r = run_bass_kernel_spmd(nc, [arrays], core_ids=[0])
    return r.results[0]["out_y"].reshape(NB, P, D)
```

```python
from contextlib import ExitStack

import numpy as np
import concourse.bass as bass
from concourse import mybir

F32 = mybir.dt.float32
BF16 = mybir.dt.bfloat16
ALU = mybir.AluOpType
ACT = mybir.ActivationFunctionType
AX_X = mybir.AxisListType.X

P = 128
D = 256
KT = D // P
HEADS = 16
HD = D // HEADS
WINDOW = 64
LN_EPS = 1e-5
FF = 768
BLOCK = 32
QMAX = 32767.0
WQMAX = 7.0
SIG_LEVELS = 65536.0
SCALE_FLOOR = 1e-12
ROUND = 12582912.0
MASKED = -1e38
ONE_PAIR = float(np.array([0x3F803F80], np.uint32).view(np.float32)[0])

NB = 16
TOK = NB * P
CB = 4
NCH = NB // CB
CT = CB * P
HU = HEADS // 2
UPI = 8
ITERS = NB * 2 // UPI
SLOTS = UPI // 2
SPLIT = 3
COMBOS = [(0, 1), (0, 0), (0, 2), (1, 0), (1, 1), (2, 0)]
STACK = len(COMBOS) * HD
NEG = STACK
VW = HD + 1
FT = FF // P
HALF = TOK // 2
DVE_NORMS = 8
W_PIECES_GU = 2 * FT * D // FF
POOL_ROW = 3

UNIT_HEADS = [[[HU * half + i for i in range(HU)] for half in range(2)],
              [[4 * (i % 4) + 2 * half + i // 4 for i in range(HU)] for half in range(2)]]


def stack_rows(side, part):
    at = [i for i, c in enumerate(COMBOS) if c[side] == part]
    step = at[1] - at[0] if len(at) > 1 else 1
    assert at == list(range(at[0], at[-1] + 1, step))
    return at[0], step, len(at)


def decoder_layer(nc, x, ctxT, wqkvT, woT, gamma, beta, xqT, xkT, xvT, w_gate, w_up, w_down, out):
    stacks = [[nc.dram_tensor(f"stack_{l}_{s}", [len(COMBOS), D, TOK], BF16, kind="Internal").ap()
               for s in range(2)] for l in range(2)]
    x_v = x.rearrange("(b p) d -> p b d", p=P)
    out_v = out.rearrange("(b p) d -> p b d", p=P)

    with ExitStack() as ctx:
        def sb(name, shape, dt=F32):
            return ctx.enter_context(nc.sbuf_tensor(name, shape, dt))

        def sem(name):
            return ctx.enter_context(nc.semaphore(name))

        resid = sb("resid", [P, NB, D])
        y = sb("y", [P, NB, D])
        w_qkv = sb("w_qkv", [P, KT, 3 * D])
        w_o = sb("w_o", [P, KT, D])
        w_x = sb("w_x", [P, 3, KT, D])
        gam = sb("gam", [P, KT])
        bet = sb("bet", [P, KT])
        w_gu = sb("w_gu", [P, 2 * FT, D])
        w_dn = sb("w_dn", [P, KT, FF])
        w_guT = sb("w_guT", [P, KT, 2 * FF])
        w_dnT = sb("w_dnT", [P, FT, D])
        x_intT = sb("x_intT", [P, KT, TOK])
        ident = sb("ident", [P, P])
        ident_b = sb("ident_b", [P, P], BF16)
        band = sb("band", [P, 4, P], BF16)
        zero = sb("zero", [P, HU])
        eps = sb("eps", [P, 1])
        rounder = sb("rounder", [P, 1])
        unrounder = sb("unrounder", [P, 1])
        stats = sb("stats", [P, NB, 6])
        mv = sb("mv", [P, NB, 2])
        sd = sb("sd", [P, NB])
        rstd = sb("rstd", [P, NB])
        nmr = sb("nmr", [P, NB])
        negm = sb("negm", [P, 4, HU])
        mparts = sb("mparts", [P, 4, SPLIT * HU], BF16)
        mrest = sb("mrest", [P, HU])
        m_T = sb("m_T", [SPLIT * HU, 4, P], BF16)
        attn = sb("attn", [P, 2, D])
        attnT = sb("attnT", [P, KT, P])
        rec = sb("rec", [P, 2, HEADS])
        o_tr = sb("o_tr", [P, 2 * P * 2])
        ablk = sb("ablk", [P, 2 * FT * 8 + KT * 24])
        wscale = sb("wscale", [P, 2 * FT * 8 + KT * 24])
        winv = sb("winv", [P, 2 * FT * 8 + KT * 24])
        rrange = sb("rrange", [P, 2, NB])
        yrange = sb("yrange", [P, 2, NB])
        gmax = sb("gmax", [P, 2 * FT])
        umax = sb("umax", [P, FT])
        pmax = sb("pmax", [P, FT])
        omax = sb("omax", [P, FT])
        sc = sb("sc", [P, 32])

        arena_g = sb("arena_g", [P, FT * TOK])
        arena_u = sb("arena_u", [P, FT * TOK])
        gate = arena_g[:, :].rearrange("p (f k) -> p f k", f=FT)
        up = arena_u[:, :].rearrange("p (f k) -> p f k", f=FT)
        used = {"g": 0, "u": 0}

        def carve(which, words, dt=F32):
            a = {"g": arena_g, "u": arena_u}[which]
            at = used[which]
            used[which] = at + words
            assert at + words <= FT * TOK
            v = a[:, at:at + words]
            return v if dt == F32 else v.bitcast(dt)

        q_stk = carve("g", SLOTS * HEADS * P // 2, BF16).rearrange("p (s h k) -> p s h k", s=SLOTS, h=HEADS)
        k_stk = carve("g", SLOTS * HEADS * P // 2, BF16).rearrange("p (s h k) -> p s h k", s=SLOTS, h=HEADS)
        parts = carve("g", 4 * SPLIT * CT // 2, BF16).rearrange("p (j s k) -> p j s k", j=4, s=SPLIT)
        rest = carve("g", 2 * CT).rearrange("p (j k) -> p j k", j=2)
        v_all = carve("u", NB * HEADS * VW).rearrange("p (b h w) -> p b h w", b=NB, h=HEADS)
        v_slot = carve("u", SLOTS * HEADS * VW).rearrange("p (s h w) -> p s h w", s=SLOTS, h=HEADS)
        probT = carve("u", 2 * HU * P).rearrange("p (s h k) -> p s h k", s=2, h=HU)
        xT = carve("u", 2 * KT * CT).rearrange("p (s k t) -> p s k t", s=2, k=KT)
        cT = carve("u", 2 * KT * CT).rearrange("p (s k t) -> p s k t", s=2, k=KT)
        o_sb = carve("u", 2 * 2 * P).rearrange("p (s k) -> p s k", s=2)
        sig = y[:, :, :].rearrange("p (s b) d -> p s (b d)", s=2)

        bank = ctx.enter_context(nc.psum_tensor("bank", [P, 8, 512], F32))
        ps_s = bank[:, 0:2, :].rearrange("p b (h k) -> p (b h) k", h=4)
        ps_st = bank[:, 2:4, :].rearrange("p b (h k) -> p (b h) k", h=4)
        ps_pv = bank[:, 4, 0:2 * P]
        ps_ot = bank[:, 5, 0:2 * P]
        ps_mt = bank[:, 6, 0:P // 2].bitcast(BF16)
        ps_ap = bank[:, 7, :]

        x_landed = [sem(f"x_landed{c}") for c in range(NCH)]
        w1_landed = sem("w1_landed")
        w2_landed = sem("w2_landed")
        wf_landed = sem("wf_landed")
        ctx_landed = [sem(f"ctx_landed{i}") for i in range(2)]
        out_landed = sem("out_landed")
        consts = sem("consts")
        pool_init = sem("pool_init")
        band_half = sem("band_half")

        def layer_semaphores(l):
            names = ("xT_t", "xT_ready", "proj_done", "v_done", "v_ready", "hi_ready", "rest_ready", "mid_ready",
                     "lo_ready", "scores_done", "max_done", "mchain", "mparts_ready", "mT_done", "mT_ready",
                     "scoresT_done", "exp_done", "pv_done", "o_ready", "oT_done", "rec_ready", "norm_done",
                     "aT_done", "aT_ready", "outp_done", "resid_done", "stats_done", "mv_done",
                     "pv_zero")
            sems = {n: sem(f"l{l}_{n}") for n in names}
            sems["stored"] = [sem(f"l{l}_stored{j}") for j in range(4)]
            sems["qk_landed"] = [sem(f"l{l}_qk_landed{j}") for j in range(SLOTS)]
            sems["v_landed"] = [sem(f"l{l}_v_landed{j}") for j in range(SLOTS)]
            sems["neg_landed"] = [sem(f"l{l}_neg_landed{j}") for j in range(2)]
            return sems

        L = [layer_semaphores(l) for l in range(2)]

        bn_done = sem("bn_done")
        ln_stats = sem("ln_stats")
        ln_sd = sem("ln_sd")
        ln_link = sem("ln_link")
        ln_coef = sem("ln_coef")
        applied = [[sem(f"applied{r}_{c}") for c in range(NCH)] for r in range(2)]
        ln_apply = sem("ln_apply")
        ln_add = sem("ln_add")
        wq_link = sem("wq_link")
        wq_done = sem("wq_done")
        ones_set = sem("ones_set")
        row_range = sem("row_range")
        y_extent = sem("y_extent")
        w_t = sem("w_t")
        w_ready = sem("w_ready")
        dve_link = sem("dve_link")
        red_in = sem("red_in")
        pool_apply = sem("pool_apply")
        red_out = sem("red_out")
        scale_ready = sem("scale_ready")
        xq = sem("xq")
        xq_t = sem("xq_t")
        xq_ready = sem("xq_ready")
        ff_done = sem("ff_done")
        ff_evac = sem("ff_evac")
        ff_abs = sem("ff_abs")
        g_round = sem("g_round")
        g_int = sem("g_int")
        sig_done = sem("sig_done")
        sig_round = sem("sig_round")
        sig_int = sem("sig_int")
        gs_done = sem("gs_done")
        gs_abs = sem("gs_abs")
        u_round = sem("u_round")
        u_int = sem("u_int")
        gs_round = sem("gs_round")
        gs_int = sem("gs_int")
        o_done = sem("o_done")
        o_pool = sem("o_pool")
        table_loaded = sem("table_loaded")
        first_done = sem("first_done")
        o_abs = sem("o_abs")
        o_round = sem("o_round")
        o_int = sem("o_int")
        down_done = sem("down_done")
        y_done = sem("y_done")

        block = ctx.enter_context(nc.Block())

        def when(eng, s, value):
            if not isinstance(value, int) or value > 0:
                eng.wait_ge(s, value)

        def run_steps(eng, step, before, after):
            for u in range(-before, UPI):
                step(0, u, lambda k: k >= 0)
            with eng.Fori(1, ITERS - 1) as it:
                for u in range(UPI):
                    step(it, u, lambda k: True)
            for u in range(UPI + after):
                step(ITERS - 1, u, lambda k: k < UPI)

        def ff_pair(m):
            return (m % FT, m // FT) if m < 2 * FT else (m // 2, m % 2)

        def ff_dst(m):
            row, half = ff_pair(m)
            return (gate if row < FT else up)[:, row % FT, half * HALF:(half + 1) * HALF]

        def apply_norm(eng, rnd, c):
            src = resid if rnd == 0 else y
            eng.wait_ge(ln_coef, LN_ORDER.index((rnd, c)) + 1)
            if rnd == 1:
                eng.wait_ge(ln_add, CB * (c + 1))
            for b in range(c * CB, (c + 1) * CB):
                eng.tensor_scalar(y[:, b, :], src[:, b, :], rstd[:, b:b + 1], nmr[:, b:b + 1], ALU.mult, ALU.add)\
                   .then_inc(applied[rnd][c], 1)

        PARTS_OF = [[0, 1, 2, 3], [2, 3, 0, 1]]

        @block.sync
        def _(sp):
            for c in range(NCH):
                sp.dma_start(resid[:, c * CB:(c + 1) * CB, :], x_v[:, c * CB:(c + 1) * CB, :]).then_inc(x_landed[c], 16)
                if c == 0:
                    sp.dma_start(w_qkv[:, :, :], wqkvT.rearrange("(k p) n -> p k n", p=P)).then_inc(w1_landed, 16)
                    sp.dma_start(gam[:, :], gamma).then_inc(w1_landed, 16)
                    sp.dma_start(bet[:, :], beta).then_inc(w1_landed, 16)
            sp.dma_start(w_o[:, :, :], woT.rearrange("(k p) n -> p k n", p=P)).then_inc(w2_landed, 16)
            for i, w in enumerate((xqT, xkT, xvT)):
                sp.dma_start(w_x[:, i, :, :], w.rearrange("(k p) n -> p k n", p=P)).then_inc(w2_landed, 16)
            sp.dma_start(w_gu[:, 0:FT, :], w_gate.rearrange("(f p) n -> p f n", p=P)).then_inc(wf_landed, 16)
            sp.dma_start(w_gu[:, FT:2 * FT, :], w_up.rearrange("(f p) n -> p f n", p=P)).then_inc(wf_landed, 16)
            sp.dma_start(w_dn[:, :, :], w_down.rearrange("(f p) n -> p f n", p=P)).then_inc(wf_landed, 16)

            def load_ctx(c):
                if c >= 2:
                    sp.wait_ge(L[1]["proj_done"], 4 * (c - 2) + 2)
                    sp.wait_ge(L[1]["v_done"], 2 * (c - 2) + 2)
                sp.dma_start(cT[:, c % 2, :, :], ctxT[:, c * CT:(c + 1) * CT].rearrange("(k p) n -> p k n", p=P))\
                  .then_inc(ctx_landed[c % 2], 16)

            load_ctx(0)
            load_ctx(1)

            def store_parts(l, c, which=range(4)):
                s = L[l]
                for pos in which:
                    j = PARTS_OF[l][pos]
                    n = 4 * c + pos
                    side, t = j // 2, j % 2
                    for part, ready in enumerate((s["hi_ready"], s["mid_ready"], s["lo_ready"])):
                        sp.wait_ge(ready, n + 1)
                        a, step, k = stack_rows(side, part)
                        dst = stacks[l][side][a:a + (k - 1) * step + 1:step, t * P:(t + 1) * P, c * CT:(c + 1) * CT]
                        sp.dma_start(dst.rearrange("c f k -> f c k"),
                                     parts[:, j, part:part + 1, :].to_broadcast([P, k, CT])).then_inc(s["stored"][j], 16)

            def stack_of(l, side, at):
                return stacks[l][side][:, :, at].rearrange("c (d h) k -> (c d) h k", h=HEADS)

            def load_side(l, side, b, slot):
                sp.dma_start((q_stk, k_stk)[side][0:STACK, slot, :, :], stack_of(l, side, bass.ds(b * P, P)))\
                  .then_inc(L[l]["qk_landed"][slot], 16)

            def load_qk(l, b, slot):
                load_side(l, 0, b, slot)
                load_side(l, 1, b, slot)

            def load_v(l, b, slot):
                sp.dma_start(v_slot[:, slot, :, :], v_all[:, bass.ds(b, 1), :, :].rearrange("p b h w -> p (b h) w"))\
                  .then_inc(L[l]["v_landed"][slot], 16)

            def attention(l):
                s = L[l]

                def step(it, u, exists):
                    if exists(u + 2):
                        sp.wait_ge(s["mT_ready"], it * UPI + u + 3)
                        v = u + 2
                        sp.dma_start(q_stk[NEG:NEG + SPLIT, (v // 2) % SLOTS, HU * (v % 2):HU * (v % 2) + HU, :],
                                     m_T[:, v % 4, :]).then_inc(s["neg_landed"][v % 2], 16)
                    for side, w in enumerate((u, u - 1)):
                        if w % 2 == 1 and exists(w) and exists(w + UPI) and w >= -1 and u >= 0:
                            if side == 0:
                                for j in range(4):
                                    sp.wait_ge(s["stored"][j], 16 * SPLIT * (2 if isinstance(it, int) else NCH))
                                sp.wait_ge(s["scoresT_done"], it * UPI + u + 1)
                            load_side(l, side, it * SLOTS + (w // 2 + SLOTS), w // 2 % SLOTS)
                    w = u - 2
                    if u >= 0 and w % 2 == 1 and exists(w) and exists(w + UPI):
                        sp.wait_ge(s["v_ready"], 2 * NCH)
                        sp.wait_ge(s["pv_done"], it * UPI + w + 1)
                        load_v(l, it * SLOTS + (w // 2 + SLOTS), w // 2 % SLOTS)
                    if isinstance(it, int) and it == 0:
                        if u in (-2, -1):
                            load_qk(l, u + 4, u + 4)
                            load_v(l, u + 4, u + 4)
                        elif u in (0, 2, 4, 6):
                            store_parts(l, NCH - 1, [u // 2])

                run_steps(sp, step, 3, 0)

            for l in range(2):
                s = L[l]
                for c in range(NCH - 1):
                    store_parts(l, c)
                    if l == 1 and c + 2 < NCH:
                        load_ctx(c + 2)
                for j in range(4):
                    sp.wait_ge(s["stored"][j], 16 * SPLIT)
                sp.wait_ge(s["v_ready"], 2)
                if l == 1:
                    sp.wait_ge(L[0]["pv_done"], 2 * NB)
                for b in range(2):
                    load_qk(l, b, b)
                    load_v(l, b, b)
                attention(l)
            for c in range(NCH):
                for a, b in ([(c * CB, (c + 1) * CB)] if c + 1 < NCH else [(c * CB, NB - 1), (NB - 1, NB)]):
                    sp.wait_ge(y_done, b)
                    sp.dma_start(out_v[:, a:b, :], resid[:, a:b, :]).then_inc(out_landed, 16)
            sp.wait_ge(out_landed, 16 * (NCH + 1))

        @block.gpsimd
        def _(pool):
            pool.memset(ident[:, :], 0.0).then_inc(pool_init, 1)
            pool.memset(ident_b[:, :], 0.0).then_inc(pool_init, 1)
            pool.memset(band[:, :, :], 0.0).then_inc(pool_init, 1)
            pool.wait_ge(pool_init, 3)
            for m in (ident, ident_b):
                pool.affine_select(out=m[:, :], in_=m[:, :], compare_op=ALU.not_equal, fill=1.0, base=0,
                                   pattern=[[-1, P]], channel_multiplier=1).then_inc(consts, 1)
            for sign in (1, -1):
                pool.affine_select(out=band[:, :, :], in_=band[:, :, :], compare_op=ALU.is_ge, fill=MASKED,
                                   base=WINDOW // 2, pattern=[[0, 4], [sign, P]], channel_multiplier=-sign)\
                    .then_inc(band_half if sign == 1 else consts, 1)
                if sign == 1:
                    pool.wait_ge(band_half, 1)
            pool.wait_ge(consts, 5)

            def add_residual(c):
                pool.wait_ge(applied[0][c], CB)
                for b in range(c * CB, (c + 1) * CB):
                    pool.tensor_tensor(resid[:, b, :], resid[:, b, :], y[:, b, :], ALU.add).then_inc(ln_add, 1)

            def mid_parts(l, c):
                for pos, j in enumerate(PARTS_OF[l]):
                    n = 4 * c + pos
                    pool.wait_ge(L[l]["rest_ready"], n + 1)
                    if c:
                        pool.wait_ge(L[l]["stored"][j], 16 * SPLIT * c)
                    pool.tensor_scalar(parts[:, j, 1, :], rest[:, n % 2, :], 1.0, 0.0, ALU.mult, ALU.add)\
                        .then_inc(L[l]["mid_ready"], 1)

            def neg_parts(l):
                s = L[l]

                def step(it, u, exists):
                    if not exists(u + 3):
                        return
                    v = u + 3
                    n = it * UPI + v
                    m = negm[:, v % 4, :]
                    to = [mparts[:, v % 4, i * HU:(i + 1) * HU] for i in range(SPLIT)]
                    pool.wait_ge(s["max_done"], n + 1)
                    pool.tensor_tensor(to[0], m, zero[:, :], ALU.add).then_inc(s["mchain"], 1)
                    pool.wait_ge(s["mchain"], n * 3 + 1)
                    pool.tensor_tensor(mrest[:, :], m, to[0], ALU.subtract).then_inc(s["mchain"], 1)
                    pool.wait_ge(s["mchain"], n * 3 + 2)
                    pool.tensor_tensor(to[1], mrest[:, :], zero[:, :], ALU.add).then_inc(s["mchain"], 1)
                    pool.wait_ge(s["mchain"], n * 3 + 3)
                    pool.tensor_tensor(to[2], mrest[:, :], to[1], ALU.subtract).then_inc(s["mparts_ready"], 1)
                    pool.wait_ge(s["mparts_ready"], n + 1)

                def add(it, u, exists):
                    if l == 1 and u % 2 == 1 and exists(u - 4):
                        b = (u - 5) // 2
                        nb = it * SLOTS + b
                        pool.wait_ge(s["norm_done"], nb + 1)
                        r = resid[:, bass.ds(nb, 1), :].rearrange("p b w -> p (b w)")
                        pool.tensor_tensor(r, r, attn[:, b % 2, :], ALU.add).then_inc(s["resid_done"], 1)

                def both(it, u, exists):
                    step(it, u, exists)
                    add(it, u, exists)

                run_steps(pool, both, 3, 6)

            for kind, rnd, c in POOL_PLAN:
                if kind == "apply":
                    apply_norm(pool, rnd, c)
                elif kind == "add":
                    add_residual(c)
                else:
                    mid_parts(0, c)
            neg_parts(0)

            for c in range(NCH):
                mid_parts(1, c)
            neg_parts(1)

            def all_max(k):
                pool.wait_ge(red_in, k + 1)
                pool.partition_all_reduce(sc[:, 2 * k + 1:2 * k + 2], sc[:, 2 * k:2 * k + 1], P,
                                          bass.bass_isa.ReduceOp.max).then_inc(red_out, 1)

            def unround(v):
                return pool.tensor_scalar(v, v, 1.0, -ROUND, ALU.mult, ALU.add)

            pool.wait_ge(ln_coef, 2 * NCH + 2)
            for b in range(DVE_NORMS, NB):
                if b == DVE_NORMS + 2:
                    all_max(0)
                pool.tensor_scalar(y[:, b, :], resid[:, b, :], rstd[:, b:b + 1], nmr[:, b:b + 1], ALU.mult, ALU.add)\
                    .then_inc(pool_apply, 1)
            all_max(1)

            def gate_int(f):
                pool.wait_ge(g_round, f)
                unround(gate[:, f, :]).then_inc(g_int, 1)

            def sig_integer(f):
                v = sig[:, f % 2, :]
                pool.wait_ge(sig_done, f + 1)
                pool.tensor_scalar(v, v, SIG_LEVELS, ROUND, ALU.mult, ALU.add).then_inc(sig_round, 1)
                pool.wait_ge(sig_round, f)
                unround(v).then_inc(sig_int, 1)

            gate_int(1)
            sig_integer(1)
            gate_int(2)
            for f in range(2, FT):
                if f + 1 < FT:
                    gate_int(f + 1)
                sig_integer(f)
            all_max(2)
            all_max(3)
            for f in range(FT):
                if f == 0:
                    pool.wait_ge(first_done, 5)
                else:
                    pool.wait_ge(gs_round, f)
                unround(gate[:, f, :]).then_inc(gs_int, 1)
                if f == POOL_ROW:
                    pool.wait_ge(u_round, f + 1)
                    unround(up[:, f, :]).then_inc(u_int, 1)
                    pool.wait_ge(gs_int, f + 1)
                    pool.wait_ge(u_int, 1)
                    pool.tensor_tensor(up[:, f, :], up[:, f, :], gate[:, f, :], ALU.mult).then_inc(o_pool, 1)
            all_max(4)

        @block.scalar
        def _(act):
            act.wait_ge(consts, 5)

            def sqrt_var(rnd, c):
                a, b = c * CB, (c + 1) * CB
                act.wait_ge(ln_stats, CB * (LN_ORDER.index((rnd, c)) + 1))
                act.activation(sd[:, a:b], mv[:, a:b, 1], ACT.Sqrt, bias=eps[:, 0:1]).then_inc(ln_sd, 1)

            def evac_xT(l, c):
                s = L[l]
                act.wait_ge(s["xT_t"], c + 1)
                if c >= 2:
                    act.wait_ge(s["proj_done"], 4 * (c - 1))
                    if l == 0:
                        act.wait_ge(s["v_done"], 2 * (c - 1))
                for k in range(KT):
                    if l == 0:
                        act.activation(xT[:, c % 2, k, :], bank[:, k, :], ACT.Identity, scale=gam[:, k:k + 1],
                                       bias=bet[:, k:k + 1]).then_inc(s["xT_ready"], 1)
                    else:
                        act.activation(xT[:, c % 2, k, :], bank[:, k, :], ACT.Copy).then_inc(s["xT_ready"], 1)

            def hi_parts(l, c, which):
                s = L[l]
                for pos, j in enumerate(PARTS_OF[l]):
                    if pos in which:
                        n = 4 * c + pos
                        act.wait_ge(s["proj_done"], n + 1)
                        if c:
                            act.wait_ge(s["stored"][j], 16 * SPLIT * c)
                        act.activation(parts[:, j, 0, :], bank[:, 2 + j, :], ACT.Copy).then_inc(s["hi_ready"], 1)

            def evac_v(l, c):
                s = L[l]
                for i in range(2):
                    b = c * CB + 2 * i
                    act.wait_ge(s["v_done"], 2 * c + i + 1)
                    act.activation(v_all[:, b:b + 2, :, 0:HD],
                                   bank[:, 6 + i, :].rearrange("p (b h w) -> p b h w", b=2, h=HEADS),
                                   ACT.Copy).then_inc(s["v_ready"], 1)

            def attention(l):
                s = L[l]

                def step(it, u, exists):
                    n = it * UPI + u
                    if u >= 0 and exists(u):
                        act.wait_ge(s["scoresT_done"], n + 1)
                        if exists(u - 2):
                            act.wait_ge(s["pv_done"], n - 1)
                        act.activation(probT[:, u % 2, :, :], ps_st, ACT.Exp, scale=HD ** -0.5)\
                            .then_inc(s["exp_done"], 1)
                    if l == 0 and exists(u - 1):
                        act.wait_ge(s["pv_done"], n)
                        if exists(u - 3):
                            act.wait_ge(s["oT_done"], n - 2)
                        act.activation(o_sb[:, (u - 1) % 2, :], ps_pv, ACT.Copy).then_inc(s["o_ready"], 1)
                    if exists(u + 2):
                        v = u + 2
                        act.wait_ge(s["mT_done"], n + 3)
                        act.activation(m_T[:, v % 4, :], ps_mt[0:SPLIT * HU, :], ACT.Copy).then_inc(s["mT_ready"], 1)
                    if l == 0 and u % 2 == 0 and exists(u - 4):
                        act.wait_ge(s["aT_done"], it * SLOTS + (u - 4) // 2 + 1)
                        act.activation(attnT[:, :, :], ps_ap[:, 0:D].rearrange("p (k t) -> p k t", k=KT), ACT.Copy)\
                            .then_inc(s["aT_ready"], 1)

                run_steps(act, step, 3, 5)

            act.activation(sc[:, 30:31], eps[:, 0:1], ACT.Sqrt).then_inc(table_loaded, 1)
            for kind, *a in ACT_PLAN:
                if kind == "xT":
                    act.wait_ge(w1_landed, 48)
                {"sqrt": sqrt_var, "xT": evac_xT, "v": evac_v, "hi": lambda l, c: hi_parts(l, c, range(4))}[kind](*a)
            attention(0)
            act.wait_ge(L[0]["mv_done"], NB)
            act.activation(sd[:, :], mv[:, :, 1], ACT.Sqrt, bias=eps[:, 0:1]).then_inc(ln_sd, 1)
            for c in range(NCH):
                hi_parts(1, c, (0, 1))
                for evac in ((evac_xT, evac_v) if c else (evac_v, evac_xT)):
                    evac(1, c)
                hi_parts(1, c, (2, 3))
            attention(1)
            act.wait_ge(L[1]["mv_done"], NB)
            act.activation(sd[:, :], mv[:, :, 1], ACT.Sqrt, bias=eps[:, 0:1]).then_inc(ln_sd, 1)
            for i in range(9):
                act.wait_ge(w_t, i + 1)
                if i < 6:
                    k, g = i // 3, i % 3
                    dst = w_guT[:, k, g * 512:(g + 1) * 512]
                else:
                    dst = w_dnT[:, 2 * (i - 6):2 * (i - 6) + 2, :].rearrange("p f n -> p (f n)")
                act.activation(dst, bank[:, i % 8, :], ACT.Copy).then_inc(w_ready, 1)
            for c in range(NCH):
                for k in range(KT):
                    n = c * KT + k
                    act.wait_ge(xq_t, n + 1)
                    act.activation(x_intT[:, k, c * CT:(c + 1) * CT], bank[:, 4 + n % 4, :], ACT.Identity,
                                   bias=unrounder[:, 0:1]).then_inc(xq_ready, 1)

            def evac_ff(m):
                act.wait_ge(ff_done, 2 * m + 2)
                act.activation(ff_dst(m), bank[:, 2 * m % 8:2 * m % 8 + 2, :].rearrange("p b k -> p (b k)"), ACT.Copy)\
                   .then_inc(ff_evac, 1)

            def round_gate(f):
                if f == 1:
                    act.wait_ge(scale_ready, 2)
                act.activation(gate[:, f, :], gate[:, f, :], ACT.Identity, scale=sc[:, 13:14], bias=rounder[:, 0:1])\
                    .then_inc(g_round, 1)

            def sigmoid(f):
                if f == 0:
                    act.wait_ge(first_done, 2)
                else:
                    act.wait_ge(g_int, f)
                if f >= 2:
                    act.wait_ge(gs_done, f - 1)
                act.activation(sig[:, f % 2, :], gate[:, f, :], ACT.Sigmoid, scale=sc[:, 12:13]).then_inc(sig_done, 1)

            for m in range(2 * FT):
                evac_ff(m)
                if m == 0:
                    act.activation(sc[:, 31:32], zero[:, 0:1], ACT.Sigmoid).then_inc(table_loaded, 1)
            for kind, i in ACT_FF_PLAN:
                {"evac": evac_ff, "round": round_gate, "sigmoid": sigmoid}[kind](i)
            for kind, f in ACT_ROUND_PLAN:
                if kind == "up":
                    if f == 0:
                        act.wait_ge(scale_ready, 3)
                    act.activation(up[:, f, :], up[:, f, :], ACT.Identity, scale=sc[:, 15:16], bias=rounder[:, 0:1])\
                        .then_inc(u_round, 1)
                else:
                    if f == 1:
                        act.wait_ge(scale_ready, 4)
                    act.activation(gate[:, f, :], gate[:, f, :], ACT.Identity, scale=sc[:, 17:18], bias=rounder[:, 0:1])\
                        .then_inc(gs_round, 1)
            act.wait_ge(scale_ready, 5)
            for b in range(NB):
                ob = up[:, :, b * P:(b + 1) * P]
                act.activation(ob, ob, ACT.Identity, scale=sc[:, 19:20], bias=rounder[:, 0:1]).then_inc(o_round, 1)

        @block.tensor
        def _(pe):
            pe.wait_ge(consts, 5)

            def transpose_x(l, c):
                s = L[l]
                if l == 0:
                    pe.wait_ge(applied[1][c], CB)
                else:
                    pe.wait_ge(ln_apply, CB * (c + 1))
                when(pe, s["xT_ready"], KT * c)
                for k in range(KT):
                    for i in range(CB):
                        ins = pe.transpose(bank[:, k, i * P:(i + 1) * P], y[:, c * CB + i, k * P:(k + 1) * P], ident[:, :])
                ins.then_inc(s["xT_t"], 1)

            def project(l, c, which):
                s = L[l]
                for pos, j in enumerate(PARTS_OF[l]):
                    if pos not in which:
                        continue
                    n = 4 * c + pos
                    if c:
                        pe.wait_ge(s["rest_ready"], n - 3)
                    if l == 1 and j >= 2:
                        pe.wait_ge(ctx_landed[c % 2], 16 * (c // 2 + 1))
                        src = cT
                    else:
                        pe.wait_ge(s["xT_ready"], KT * (c + 1))
                        src = xT
                    for k in range(KT):
                        w = (w_qkv[:, k, j * P:(j + 1) * P] if l == 0 else
                             w_x[:, j // 2, k, (j % 2) * P:(j % 2 + 1) * P])
                        ins = pe.matmul(bank[:, 2 + j, :], w, src[:, c % 2, k, :], start=(k == 0), stop=(k == KT - 1))
                    ins.then_inc(s["proj_done"], 1)

            def values(l, c):
                s = L[l]
                src = xT if l == 0 else cT
                for i in range(CB):
                    if i % 2 == 0 and c:
                        pe.wait_ge(s["v_ready"], 2 * (c - 1) + i // 2 + 1)
                    for k in range(KT):
                        w = w_qkv[:, k, 2 * D:3 * D] if l == 0 else w_x[:, 2, k, :]
                        ins = pe.matmul(bank[:, 6 + i // 2, (i % 2) * D:(i % 2 + 1) * D],
                                        src[:, c % 2, k, i * P:(i + 1) * P], w, start=(k == 0), stop=(k == KT - 1))
                    if i % 2:
                        ins.then_inc(s["v_done"], 1)

            def attention(l):
                s = L[l]
                pe.wait_ge(s["xT_ready"], KT * NCH)
                pe.wait_ge(ones_set, 1)

                def scores(it, u):
                    slot = (u // 2) % SLOTS
                    if u % 2 == 0:
                        pe.wait_ge(s["qk_landed"][slot], (it + u // UPI) * 32 + 32)
                    if not (isinstance(it, int) and it * UPI + u == 0):
                        pe.wait_ge(s["max_done"], it * UPI + u)
                    if l == 0:
                        for g in range(2):
                            pe.matmul(bank[:, g, :], ident_b[:, :], band[:, :, :].rearrange("p h k -> p (h k)"),
                                      start=True, stop=False, skip_group_check=True)
                    for i in range(HU):
                        h = HU * (u % 2) + i
                        ins = pe.matmul(ps_s[:, i, :], q_stk[0:STACK, slot, h, :], k_stk[0:STACK, slot, h, :],
                                        start=(l == 1), stop=True, skip_group_check=True)
                    ins.then_inc(s["scores_done"], 1)

                def scores_T(it, u):
                    if isinstance(it, int) and it * UPI + u == 0:
                        pe.wait_ge(s["rest_ready"], 4 * NCH)
                    slot = (u // 2) % SLOTS
                    pe.wait_ge(s["neg_landed"][u % 2], it * (16 * UPI // 2) + 16 * (u // 2 + 1))
                    if not (isinstance(it, int) and it * UPI + u == 0):
                        pe.wait_ge(s["exp_done"], it * UPI + u)
                    if l == 0:
                        for g in range(2):
                            pe.matmul(bank[:, 2 + g, :], ident_b[:, :], band[:, :, :].rearrange("p h k -> p (h k)"),
                                      start=True, stop=False, skip_group_check=True)
                    for i in range(HU):
                        h = HU * (u % 2) + i
                        ins = pe.matmul(ps_st[:, i, :], k_stk[0:NEG + SPLIT, slot, h, :], q_stk[0:NEG + SPLIT, slot, h, :],
                                        start=(l == 1), stop=True, skip_group_check=True)
                    ins.then_inc(s["scoresT_done"], 1)

                def weighted(it, u, has_before):
                    slot = (u // 2) % SLOTS
                    if u % 2 == 0:
                        pe.wait_ge(s["v_landed"][slot], (it + u // UPI) * 16 + 16)
                    pe.wait_ge(s["exp_done"], it * UPI + u + 1)
                    if isinstance(it, int) and it * UPI + u == 0:
                        pe.wait_ge(s["pv_zero"], l + 1)
                    if has_before:
                        if l == 0:
                            pe.wait_ge(s["o_ready"], it * UPI + u)
                        elif u % 2 == 0:
                            pe.wait_ge(s["o_ready"], it * SLOTS + u // 2 - 1)
                    for i in range(HU):
                        h = UNIT_HEADS[l][u % 2][i]
                        r = 32 * (i % 4)
                        at = i // 4 * P + (l * (u % 2) * 2 * P)
                        out_bank = 4 + l * (u // 2 % 2)
                        ins = pe.matmul(bank[r:r + VW, out_bank, at:at + P], v_slot[:, slot, h, :],
                                        probT[:, u % 2, i, :], start=True, stop=True, skip_group_check=True)
                    ins.then_inc(s["pv_done"], 1)

                def step(it, u, exists):
                    n = it * UPI + u
                    if exists(u + 3):
                        scores(it, u + 3)
                    if u >= 0 and exists(u):
                        scores_T(it, u)
                    if exists(u - 1):
                        weighted(it, u - 1, exists(u - 2) if l == 0 else exists(u - 5))
                    if exists(u + 2):
                        v = u + 2
                        pe.wait_ge(s["mparts_ready"], n + 3)
                        if isinstance(it, int) and it * UPI + v == 0:
                            pe.wait_ge(s["v_ready"], 2 * NCH)
                        if exists(u + 1):
                            pe.wait_ge(s["mT_ready"], n + 2)
                        pe.transpose(ps_mt[0:SPLIT * HU, :], mparts[:, v % 4, :], ident_b[:, :]).then_inc(s["mT_done"], 1)
                    if l == 0 and exists(u - 2):
                        v = u - 2
                        pe.wait_ge(s["o_ready"], n - 1)
                        if exists(u - 3):
                            pe.wait_ge(s["norm_done"], n - 2)
                        for g in range(2):
                            ins = pe.transpose(ps_ot[:, g * P:(g + 1) * P], o_sb[:, v % 2, g * P:(g + 1) * P], ident[:, :])
                        ins.then_inc(s["oT_done"], 1)
                    if l == 0 and u % 2 == 0 and exists(u - 4):
                        v = u - 4
                        nb = it * SLOTS + v // 2
                        pe.wait_ge(s["norm_done"], it * UPI + v + 2)
                        if exists(v - 2):
                            pe.wait_ge(s["resid_done"], nb)
                        for k in range(KT):
                            ins = pe.transpose(ps_ap[:, k * P:(k + 1) * P], attn[:, (v // 2) % 2, k * P:(k + 1) * P], ident[:, :])
                        ins.then_inc(s["aT_done"], 1)
                    if l == 0 and u % 2 == 1 and exists(u - 5):
                        nb = it * SLOTS + (u - 5) // 2
                        pe.wait_ge(s["aT_ready"], nb + 1)
                        for k in range(KT):
                            ins = pe.matmul(ps_ap[:, 0:D], attnT[:, k, :], w_o[:, k, :], start=(k == 0), stop=(k == KT - 1))
                        ins.then_inc(s["outp_done"], 1)

                run_steps(pe, step, 3, 6)

            pe.wait_ge(w1_landed, 48)
            transpose_x(0, 0)
            for c in range(NCH):
                project(0, c, range(4))
                if c + 1 < NCH:
                    transpose_x(0, c + 1)
                values(0, c)
            pe.wait_ge(w2_landed, 64)
            attention(0)
            pe.wait_ge(L[0]["max_done"], 2 * NB)
            pe.wait_ge(L[0]["exp_done"], 2 * NB)
            pe.wait_ge(L[0]["norm_done"], 2 * NB)
            for c in range(NCH):
                project(1, c, (0, 1))
                if c:
                    transpose_x(1, c)
                    values(1, c)
                else:
                    pe.wait_ge(L[0]["resid_done"], NB)
                    values(1, c)
                    transpose_x(1, c)
                project(1, c, (2, 3))
            attention(1)
            pe.wait_ge(L[1]["resid_done"], NB)
            pe.wait_ge(wq_done, 3 * (W_PIECES_GU + KT))
            for i in range(9):
                if i == 8:
                    pe.wait_ge(w_ready, 1)
                for j in range(4):
                    if i < 6:
                        k, f = i // 3, (i % 3) * 4 + j
                        src = w_gu[:, f, k * P:(k + 1) * P]
                    else:
                        f, k = 2 * (i - 6) + j // 2, j % 2
                        src = w_dn[:, k, f * P:(f + 1) * P]
                    ins = pe.transpose(bank[:, i % 8, j * P:(j + 1) * P], src, ident[:, :])
                ins.then_inc(w_t, 1)

            def transpose_xq(c):
                pe.wait_ge(xq, c + 1)
                for k in range(KT):
                    n = c * KT + k
                    if n < 4:
                        pe.wait_ge(w_ready, 5 + n)
                    else:
                        pe.wait_ge(xq_ready, n - 3)
                    for i in range(CB):
                        ins = pe.transpose(bank[:, 4 + n % 4, i * P:(i + 1) * P], y[:, c * CB + i, k * P:(k + 1) * P], ident[:, :])
                    ins.then_inc(xq_t, 1)

            transpose_xq(0)
            transpose_xq(1)
            pe.wait_ge(w_ready, 9)
            for n in range(2 * FT * NCH):
                row, half = ff_pair(n // 2)
                c = 2 * half + n % 2
                if n < 2:
                    pe.wait_ge(xq_ready, KT * (c + 1))
                if n == 2:
                    transpose_xq(2)
                    transpose_xq(3)
                if n == 4:
                    pe.wait_ge(xq_ready, KT * NCH)
                if n >= 8 and n % 2 == 0:
                    pe.wait_ge(ff_evac, n // 2 - 3)
                for k in range(KT):
                    ins = pe.matmul(bank[:, n % 8, :], w_guT[:, k, row * P:(row + 1) * P],
                                    x_intT[:, k, c * CT:(c + 1) * CT], start=(k == 0), stop=(k == KT - 1))
                ins.then_inc(ff_done, 1)
            pe.wait_ge(ff_evac, 4 * FT)
            for b in range(NB):
                pe.wait_ge(o_int, b + 1)
                if b >= 8:
                    pe.wait_ge(y_done, b - 7)
                for f in range(FT):
                    ins = pe.matmul(bank[:, b % 8, 0:D], up[:, f, b * P:(b + 1) * P], w_dnT[:, f, :],
                                    start=(f == 0), stop=(f == FT - 1))
                ins.then_inc(down_done, 1)

        @block.vector
        def _(dve):
            dve.memset(eps[:, :], LN_EPS).then_inc(dve_link, 1)
            dve.memset(rounder[:, :], ROUND).then_inc(dve_link, 1)
            dve.memset(unrounder[:, :], -ROUND).then_inc(dve_link, 1)
            dve.memset(v_all[:, :, :, HD:VW], 1.0).then_inc(consts, 1)
            dve.memset(zero[:, :], 0.0).then_inc(consts, 1)
            dve.memset(k_stk[NEG:NEG + SPLIT, :, :, :].bitcast(F32), ONE_PAIR).then_inc(ones_set, 1)
            dve.wait_ge(dve_link, 3)
            chain = [3]

            def link(ins):
                chain[0] += 1
                ins.then_inc(dve_link, 1)
                dve.wait_ge(dve_link, chain[0])

            def norm_stats(rnd, c):
                src = resid if rnd == 0 else y
                k = LN_ORDER.index((rnd, c))
                if rnd == 0:
                    dve.wait_ge(x_landed[c], 16)
                else:
                    dve.wait_ge(applied[0][c], CB)
                    dve.wait_ge(ln_coef, LN_ORDER.index((0, c)) + 1)
                for b in range(c * CB, (c + 1) * CB):
                    dve.bn_stats(stats[:, b, :], src[:, b, :]).then_inc(bn_done, 1)
                dve.wait_ge(bn_done, CB * (k + 1))
                for b in range(c * CB, (c + 1) * CB):
                    dve.bn_aggr(mv[:, b, :], stats[:, b, :]).then_inc(ln_stats, 1)

            def norm_coef(k, a, b):
                dve.wait_ge(ln_sd, k + 1)
                dve.reciprocal(rstd[:, a:b], sd[:, a:b]).then_inc(ln_link, 1)
                dve.wait_ge(ln_link, k + 1)
                dve.scalar_tensor_tensor(out=nmr[:, a:b], in0=mv[:, a:b, 0], scalar=-1.0, in1=rstd[:, a:b],
                                         op0=ALU.mult, op1=ALU.mult).then_inc(ln_coef, 1)

            def low_part(l, n):
                s = L[l]
                j = PARTS_OF[l][n % 4]
                dve.wait_ge(s["mid_ready"], n + 1)
                dve.tensor_tensor(parts[:, j, 2, :], rest[:, n % 2, :], parts[:, j, 1, :], ALU.subtract)\
                   .then_inc(s["lo_ready"], 1)

            def split(l, c, which):
                s = L[l]
                for pos, j in enumerate(PARTS_OF[l]):
                    if pos not in which:
                        continue
                    n = 4 * c + pos
                    dve.wait_ge(s["hi_ready"], n + 1)
                    if n >= 2:
                        dve.wait_ge(s["lo_ready"], n - 1)
                    dve.tensor_tensor(rest[:, n % 2, :], bank[:, 2 + j, :], parts[:, j, 0, :], ALU.subtract)\
                       .then_inc(s["rest_ready"], 1)
                    if n:
                        low_part(l, n - 1)

            def residual_stats(s, nb):
                dve.wait_ge(s["resid_done"], nb + 1)
                dve.bn_stats(stats[:, bass.ds(nb, 1), :], resid[:, bass.ds(nb, 1), :]).then_inc(s["stats_done"], 1)

            def all_moments(s):
                dve.wait_ge(s["stats_done"], NB)
                for b in range(NB):
                    dve.bn_aggr(mv[:, b, :], stats[:, b, :]).then_inc(s["mv_done"], 1)

            def attention(l):
                s = L[l]
                dve.wait_ge(s["rest_ready"], 4 * NCH)
                dve.wait_ge(s["proj_done"], 4 * NCH)

                def step(it, u, exists):
                    n = it * UPI + u
                    if exists(u + 3):
                        v = u + 3
                        dve.wait_ge(s["scores_done"], n + 4)
                        dve.tensor_reduce(negm[:, v % 4, :], ps_s, AX_X, ALU.max, negate=True).then_inc(s["max_done"], 1)
                    if l == 0 and exists(u - 2):
                        v = u - 2
                        hs = HU * (v % 2)
                        dve.wait_ge(s["oT_done"], n - 1)
                        ot = ps_ot.rearrange("p (h w) -> p h w", h=HU)
                        dve.reciprocal(rec[:, v % 2, 0:HU], ot[:, :, HD]).then_inc(s["rec_ready"], 1)
                        dve.wait_ge(s["rec_ready"], n - 1)
                        if exists(v - 4):
                            dve.wait_ge(s["aT_done"], it * SLOTS + v // 2 - 1)
                        dst = attn[:, (v // 2) % 2, hs * HD:(hs + HU) * HD]
                        dve.tensor_tensor(dst.rearrange("p (h w) -> p h w", h=HU), ot[:, :, 0:HD],
                                          rec[:, v % 2, 0:HU].unsqueeze(2).to_broadcast([P, HU, HD]), ALU.mult)\
                           .then_inc(s["norm_done"], 1)
                    if l == 1 and u % 2 == 1:
                        b = (u - 3) // 2
                        nb = it * SLOTS + b
                        if exists(u - 2):
                            dve.wait_ge(s["pv_done"], it * UPI + u - 1)
                            if exists(u - 4):
                                dve.wait_ge(s["norm_done"], nb)
                            src = bank[:, 4 + b % 2, :].rearrange("p (g j i) -> p i g j", g=4, j=HU)
                            dve.transpose(o_tr[:, :], src).then_inc(s["o_ready"], 1)
                        if exists(u - 7):
                            dve.wait_ge(s["resid_done"], nb - 1)
                            dve.bn_stats(stats[:, bass.ds(nb - 2, 1), :], resid[:, bass.ds(nb - 2, 1), :])\
                               .then_inc(s["stats_done"], 1)
                        if exists(u - 2):
                            dve.wait_ge(s["o_ready"], nb + 1)
                            dve.reciprocal(rec[:, 0, :], o_tr[:, :].rearrange("p (i w) -> p i w", w=32)[:, :, HD])\
                               .then_inc(s["rec_ready"], 1)
                    if l == 1 and u % 2 == 0:
                        b = (u - 4) // 2
                        nb = it * SLOTS + b
                        if exists(u - 3):
                            dve.wait_ge(s["rec_ready"], nb + 1)
                            ot = o_tr[:, :].rearrange("p (i w) -> p i w", w=32)
                            dve.tensor_tensor(attn[:, b % 2, :].rearrange("p (i w) -> p i w", w=HD), ot[:, :, 0:HD],
                                              rec[:, 0, :].unsqueeze(2).to_broadcast([P, HEADS, HD]), ALU.mult)\
                               .then_inc(s["norm_done"], 1)
                        if exists(u - 8):
                            rows = resid[:, bass.ds(nb - 2, 1), :]
                            for i, op in enumerate((ALU.max, ALU.min)):
                                dve.tensor_reduce(rrange[:, i, bass.ds(nb - 2, 1)], rows, AX_X, op).then_inc(row_range, 1)
                    if l == 0 and u % 2 == 1 and exists(u - 5):
                        nb = it * SLOTS + (u - 5) // 2
                        dve.wait_ge(s["outp_done"], nb + 1)
                        r = resid[:, bass.ds(nb, 1), :].rearrange("p b w -> p (b w)")
                        dve.tensor_tensor(r, ps_ap[:, 0:D], r, ALU.add).then_inc(s["resid_done"], 1)
                        residual_stats(s, nb)

                def both(it, u, exists):
                    step(it, u, exists)
                    if u == -3:
                        low_part(l, 4 * NCH - 1)
                    if u == -1:
                        for i in range(l + 1):
                            dve.memset(bank[:, 4 + i, :], 0.0).then_inc(s["pv_zero"], 1)
                    if l == 0 and isinstance(it, int) and it * UPI + u >= 0:
                        k = u if it == 0 else UPI + u
                        if k < 2:
                            weight_scales(k + 1)
                        for i in (2 * (k - 2), 2 * (k - 2) + 1):
                            if 0 <= i < 3 * (W_PIECES_GU + KT):
                                quantise_weights(i)

                run_steps(dve, both, 3, 6)
                if l == 1:
                    for i, op in enumerate((ALU.max, ALU.min)):
                        dve.tensor_reduce(rrange[:, i, NB - 1:NB], resid[:, NB - 1, :], AX_X, op).then_inc(row_range, 1)

            W_PIECES = [(w_gu[:, 0:FT, :], 0), (w_gu[:, FT:2 * FT, :], FT * 8), (w_dn[:, :, :], 2 * FT * 8)]

            def weight_scales(i):
                w, at = W_PIECES[i]
                n = w.shape[1] * w.shape[2] // BLOCK
                if i == 0:
                    dve.wait_ge(wf_landed, 48)
                dve.tensor_reduce(ablk[:, at:at + n], w.rearrange("p f (g e) -> p (f g) e", e=BLOCK), AX_X,
                                  ALU.max, apply_absolute_value=True).then_inc(wq_link, 1)
                dve.wait_ge(wq_link, 3 * i + 1)
                dve.tensor_scalar(wscale[:, at:at + n], ablk[:, at:at + n], 1.0 / WQMAX, SCALE_FLOOR, ALU.mult, ALU.max)\
                   .then_inc(wq_link, 1)
                dve.wait_ge(wq_link, 3 * i + 2)
                dve.reciprocal(winv[:, at:at + n], wscale[:, at:at + n]).then_inc(wq_link, 1)

            def quantise_weights(i):
                piece, stage = i // 3, i % 3
                w = w_gu[:, 3 * piece:3 * piece + 3, :] if piece < W_PIECES_GU else w_dn[:, piece - W_PIECES_GU:piece - W_PIECES_GU + 1, :]
                n = FF // BLOCK
                by = (winv, None, wscale)[stage]
                wv = w.rearrange("p f (g e) -> p (f g) e", e=BLOCK)
                if i == 0:
                    dve.wait_ge(wq_link, 9)
                else:
                    dve.wait_ge(wq_done, i)
                if stage == 1:
                    dve.tensor_scalar(wv, wv, ROUND, -ROUND, ALU.add, ALU.add).then_inc(wq_done, 1)
                else:
                    dve.tensor_tensor(wv, wv, by[:, piece * n:(piece + 1) * n].unsqueeze(2).to_broadcast([P, n, BLOCK]),
                                      ALU.mult).then_inc(wq_done, 1)

            for kind, *a in DVE_PLAN:
                if kind == "stats":
                    norm_stats(*a)
                elif kind == "coef":
                    rnd, c = a
                    norm_coef(LN_ORDER.index((rnd, c)), c * CB, (c + 1) * CB)
                elif kind == "apply":
                    apply_norm(dve, *a)
                elif kind == "wscale":
                    weight_scales(*a)
                else:
                    split(0, a[0], range(4))
            dve.wait_ge(ln_add, NB)
            attention(0)
            all_moments(L[0])
            norm_coef(2 * NCH, 0, NB)
            dve.wait_ge(ln_coef, 2 * NCH + 1)

            def apply(c):
                for b in range(c * CB, (c + 1) * CB):
                    dve.tensor_scalar(y[:, b, :], resid[:, b, :], rstd[:, b:b + 1], nmr[:, b:b + 1], ALU.mult, ALU.add)\
                       .then_inc(ln_apply, 1)

            apply(0)
            for c in range(NCH):
                split(1, c, (0, 1))
                if c + 1 < NCH:
                    apply(c + 1)
                split(1, c, (2, 3))
            attention(1)
            all_moments(L[1])
            norm_coef(2 * NCH + 1, 0, NB)
            dve.wait_ge(ln_coef, 2 * NCH + 2)
            for i in range(2):
                if i == 0:
                    dve.wait_ge(row_range, 2 * NB)
                dve.tensor_tensor(yrange[:, i, :], rrange[:, i, :], rstd[:, :], ALU.mult).then_inc(y_extent, 1)
            dve.wait_ge(y_extent, 2)
            for i in range(2):
                dve.tensor_tensor(yrange[:, i, :], yrange[:, i, :], nmr[:, :], ALU.add).then_inc(y_extent, 1)
            dve.wait_ge(y_extent, 4)

            def largest(k, cells):
                dve.tensor_reduce(sc[:, 2 * k:2 * k + 1], cells, AX_X, ALU.max, apply_absolute_value=True)\
                   .then_inc(red_in, 1)

            def quant_scale(k, cells, prefactor):
                if cells is not None:
                    largest(k, cells)
                dve.wait_ge(red_out, k + 1)
                s_, m_ = sc[:, 10 + 2 * k:11 + 2 * k], sc[:, 11 + 2 * k:12 + 2 * k]
                if prefactor is None:
                    link(dve.tensor_scalar(s_, sc[:, 2 * k + 1:2 * k + 2], 1.0 / QMAX, SCALE_FLOOR, ALU.mult, ALU.max))
                    dve.reciprocal(m_, s_).then_inc(scale_ready, 1)
                else:
                    link(dve.tensor_scalar(sc[:, 24:25], sc[:, 2 * k + 1:2 * k + 2], prefactor, 1.0 / QMAX, ALU.mult, ALU.mult))
                    link(dve.tensor_scalar(s_, sc[:, 24:25], SCALE_FLOOR, None, ALU.max))
                    link(dve.reciprocal(sc[:, 25:26], s_))
                    dve.tensor_scalar(m_, sc[:, 25:26], prefactor, None, ALU.mult).then_inc(scale_ready, 1)
                dve.wait_ge(scale_ready, k + 1)

            def quantise_x(c):
                if c < DVE_NORMS // CB:
                    dve.wait_ge(ln_apply, CB * (NCH + c + 1))
                else:
                    dve.wait_ge(pool_apply, CB * (c + 1) - DVE_NORMS)
                yc = y[:, c * CB:(c + 1) * CB, :]
                dve.tensor_scalar(yc, yc, sc[:, 11:12], ROUND, ALU.mult, ALU.add).then_inc(xq, 1)

            largest(0, yrange[:, :, :].rearrange("p i b -> p (i b)"))
            for b in range(DVE_NORMS):
                if b == CB:
                    quant_scale(0, None, None)
                dve.tensor_scalar(y[:, b, :], resid[:, b, :], rstd[:, b:b + 1], nmr[:, b:b + 1], ALU.mult, ALU.add)\
                   .then_inc(ln_apply, 1)
                if b == CB:
                    quantise_x(0)
            for c in range(1, NCH):
                quantise_x(c)

            def row_max(cells, v, f, done):
                dve.tensor_reduce(cells[:, f:f + 1], v[:, f, :], AX_X, ALU.max, apply_absolute_value=True).then_inc(done, 1)

            def up_max(f):
                dve.wait_ge(ff_evac, 2 * FT + 2 * f + 2)
                row_max(umax, up, f, ff_abs)

            for m in range(2 * FT):
                dve.wait_ge(ff_evac, m + 1)
                dve.tensor_reduce(gmax[:, m:m + 1], ff_dst(m), AX_X, ALU.max, apply_absolute_value=True).then_inc(ff_abs, 1)
            dve.wait_ge(ff_abs, 2 * FT)
            quant_scale(1, gmax[:, :], sc[:, 10:11])
            link(dve.tensor_scalar(sc[:, 26:27], sc[:, 12:13], 1.0 / SIG_LEVELS, None, ALU.mult))
            dve.tensor_scalar(gate[:, 0, :], gate[:, 0, :], sc[:, 13:14], ROUND, ALU.mult, ALU.add).then_inc(first_done, 1)
            dve.wait_ge(first_done, 1)
            dve.tensor_scalar(gate[:, 0, :], gate[:, 0, :], -ROUND, None, ALU.add).then_inc(first_done, 1)
            dve.wait_ge(sig_done, 1)
            dve.tensor_scalar(sig[:, 0, :], sig[:, 0, :], SIG_LEVELS, ROUND, ALU.mult, ALU.add).then_inc(first_done, 1)
            dve.wait_ge(first_done, 3)
            dve.tensor_scalar(sig[:, 0, :], sig[:, 0, :], -ROUND, None, ALU.add).then_inc(first_done, 1)
            dve.wait_ge(first_done, 4)
            for f in range(FT):
                if f:
                    dve.wait_ge(sig_int, f)
                dve.scalar_tensor_tensor(out=gate[:, f, :], in0=sig[:, f % 2, :], scalar=SIG_LEVELS - 1, in1=gate[:, f, :],
                                         op0=ALU.min, op1=ALU.mult).then_inc(gs_done, 1)
                dve.wait_ge(gs_done, f + 1)
                row_max(pmax, gate, f, gs_abs)
                if 0 < f < FT - 1:
                    up_max(f - 1)
                if f == FT - 2:
                    up_max(FT - 2)
                    up_max(FT - 1)
                    dve.wait_ge(ff_abs, 3 * FT)
                    quant_scale(2, umax[:, :], sc[:, 10:11])
            dve.wait_ge(gs_abs, FT)
            quant_scale(3, pmax[:, :], sc[:, 26:27])
            dve.tensor_scalar(gate[:, 0, :], gate[:, 0, :], sc[:, 17:18], ROUND, ALU.mult, ALU.add).then_inc(first_done, 1)
            link(dve.tensor_scalar(sc[:, 27:28], sc[:, 14:15], sc[:, 16:17], None, ALU.mult))
            done = 0
            for f in range(FT):
                if f == POOL_ROW:
                    dve.wait_ge(o_pool, 1)
                else:
                    dve.wait_ge(u_round, f + 1)
                    dve.wait_ge(gs_int, f + 1)
                    dve.scalar_tensor_tensor(out=up[:, f, :], in0=up[:, f, :], scalar=-ROUND, in1=gate[:, f, :],
                                             op0=ALU.add, op1=ALU.mult).then_inc(o_done, 1)
                    done += 1
                    dve.wait_ge(o_done, done)
                row_max(omax, up, f, o_abs)
            dve.wait_ge(o_abs, FT)
            quant_scale(4, omax[:, :], sc[:, 27:28])

            def final(b):
                dve.wait_ge(down_done, b + 1)
                dve.scalar_tensor_tensor(out=resid[:, b, :], in0=bank[:, b % 8, 0:D], scalar=sc[:, 18:19],
                                         in1=resid[:, b, :], op0=ALU.mult, op1=ALU.add).then_inc(y_done, 1)

            for b in range(NB):
                ob = up[:, :, b * P:(b + 1) * P]
                dve.wait_ge(o_round, b + 1)
                dve.tensor_scalar(ob, ob, -ROUND, None, ALU.add).then_inc(o_int, 1)
                if b >= 3:
                    final(b - 3)
            for b in range(NB - 3, NB):
                final(b)


LN_ORDER = [(0, 0), (1, 0), (0, 1), (0, 2), (1, 1), (1, 2), (0, 3), (1, 3)]
DVE_PLAN = [("stats", 0, 0), ("coef", 0, 0), ("apply", 0, 0), ("stats", 1, 0), ("coef", 1, 0), ("apply", 1, 0),
            ("stats", 0, 1), ("coef", 0, 1), ("stats", 0, 2), ("coef", 0, 2), ("stats", 1, 1), ("coef", 1, 1),
            ("split", 0), ("wscale", 0), ("stats", 1, 2), ("coef", 1, 2), ("stats", 0, 3), ("coef", 0, 3), ("split", 1),
            ("stats", 1, 3), ("coef", 1, 3), ("apply", 1, 3), ("split", 2), ("split", 3)]
POOL_PLAN = [("add", 0, 0), ("apply", 0, 1), ("add", 0, 1), ("apply", 1, 1), ("mid", 0, 0), ("apply", 0, 2), ("add", 0, 2),
             ("apply", 1, 2), ("mid", 0, 1), ("apply", 0, 3), ("add", 0, 3), ("mid", 0, 2), ("mid", 0, 3)]
ACT_PLAN = [("sqrt", 0, 0), ("sqrt", 1, 0), ("xT", 0, 0), ("sqrt", 0, 1), ("sqrt", 0, 2), ("sqrt", 1, 1), ("hi", 0, 0),
            ("xT", 0, 1), ("v", 0, 0), ("sqrt", 1, 2), ("sqrt", 0, 3), ("hi", 0, 1), ("xT", 0, 2), ("v", 0, 1),
            ("sqrt", 1, 3), ("hi", 0, 2), ("xT", 0, 3), ("v", 0, 2), ("hi", 0, 3), ("v", 0, 3)]
ACT_FF_PLAN = [("round", 1), ("evac", 12), ("sigmoid", 0), ("sigmoid", 1), ("round", 2), ("evac", 13), ("round", 3),
               ("evac", 14), ("sigmoid", 2), ("evac", 15), ("evac", 16), ("sigmoid", 3), ("round", 4), ("evac", 17),
               ("evac", 18), ("sigmoid", 4), ("round", 5), ("evac", 19), ("sigmoid", 5), ("evac", 20), ("evac", 21),
               ("evac", 22), ("evac", 23)]
ACT_ROUND_PLAN = [("up", 0), ("up", 1), ("up", 2), ("gated", 1), ("gated", 2), ("up", 3), ("gated", 3), ("up", 4),
                  ("gated", 4), ("up", 5), ("gated", 5)]


def by_dim(w, layer):
    heads = [h for half in UNIT_HEADS[layer] for h in half]
    return w.reshape(HEADS, HD, D)[heads].transpose(2, 1, 0).reshape(D, D)


def kernel(x, ctx_1024, L0_attn_w_qkv, L0_attn_w_out, L0_attn_gamma, L0_attn_beta, L0_xattn_Wq, L0_xattn_Wk,
           L0_xattn_Wv, L0_ffn_w_gate, L0_ffn_w_up, L0_ffn_w_down):
    import concourse.bacc as bacc
    from concourse.bass_utils import run_bass_kernel_spmd

    wqkv = np.asarray(L0_attn_w_qkv)
    laid = {
        "x": np.asarray(x).reshape(TOK, D),
        "ctxT": np.asarray(ctx_1024).reshape(TOK, D).T,
        "wqkvT": np.concatenate([by_dim(wqkv[0:D], 0), by_dim(wqkv[D:2 * D], 0), wqkv[2 * D:].T], axis=1),
        "woT": np.asarray(L0_attn_w_out).T,
        "gamma": np.asarray(L0_attn_gamma).reshape(KT, P).T,
        "beta": np.asarray(L0_attn_beta).reshape(KT, P).T,
        "xqT": by_dim(np.asarray(L0_xattn_Wq), 1),
        "xkT": by_dim(np.asarray(L0_xattn_Wk), 1),
        "xvT": np.asarray(L0_xattn_Wv).T,
        "w_gate": np.asarray(L0_ffn_w_gate),
        "w_up": np.asarray(L0_ffn_w_up),
        "w_down": np.asarray(L0_ffn_w_down),
    }
    nc = bacc.Bacc("TRN2", target_bir_lowering=False, num_devices=1)
    arrays, args = {}, []
    for name, a in laid.items():
        a = np.ascontiguousarray(a)
        arrays[f"in_{name}"] = a
        args.append(nc.dram_tensor(f"in_{name}", a.shape, mybir.dt.from_np(a.dtype), kind="ExternalInput").ap())
    args.append(nc.dram_tensor("out_y", [TOK, D], F32, kind="ExternalOutput").ap())
    decoder_layer(nc, *args)
    r = run_bass_kernel_spmd(nc, [arrays], core_ids=[0])
    return r.results[0]["out_y"].reshape(NB, P, D)
```
